# Optimizing a Trainium2 kernel written in Bass

```python
import numpy as np
import jax
import jax.numpy as jnp

def _softmax(x, axis=-1):
    return jax.nn.softmax(x, axis=axis)

def _gelu(x):
    return jax.nn.gelu(x, approximate=True)

def _silu(x):
    return jax.nn.silu(x)

def _sigmoid(x):
    return jax.nn.sigmoid(x)

def _layernorm(x, axis=-1, eps=1e-05):
    m = jnp.mean(x, axis=axis, keepdims=True)
    v = jnp.var(x, axis=axis, keepdims=True)
    return (x - m) / jnp.sqrt(v + eps)

def _scatter_add(tgt, idx, src, axis=0):
    return tgt.at[idx].add(src)

def _segment_sum(src, seg, n):
    return jax.ops.segment_sum(src, seg, n)
kernel_name = 'mk_gnn_resnorm_d4_gnn_r8_6d6cba'

def setup_inputs(seed: int=0):
    np.random.seed(seed)
    _w = jnp.asarray

    def _rec_inputs():
        import jax
        import jax.numpy as jnp
        _gk = jax.random.key(seed)
        x = -0.0003713 + 1 * jax.random.normal(jax.random.fold_in(_gk, 1), (6250, 128), jnp.float32)
        _s = jax.random.randint(jax.random.fold_in(_gk, 2), (50000,), 0, 6250, jnp.int32)
        _d = jax.random.randint(jax.random.fold_in(_gk, 3), (50000,), 0, 6250, jnp.int32)
        _loop = jnp.arange(6250, dtype=jnp.int32)
        src = jnp.concatenate([_s, _d, _loop])
        dst = jnp.concatenate([_d, _s, _loop])
        _o = jnp.argsort(dst, stable=True)
        src = src[_o]
        dst = dst[_o]
        edge_attr_16 = 0.000254156 + 0.999948 * jax.random.normal(jax.random.fold_in(_gk, 12), (106250, 16), jnp.float32)
        edge_attr_4 = 0.00109026 + 0.999989 * jax.random.normal(jax.random.fold_in(_gk, 13), (106250, 4), jnp.float32)
        edge_attr_64 = 0.000103221 + 1.00003 * jax.random.normal(jax.random.fold_in(_gk, 14), (106250, 64), jnp.float32)
        node_vec1 = jax.random.uniform(jax.random.fold_in(_gk, 16), (6250, 1), jnp.float32, 0.0, 1)
        return (x, src, dst, edge_attr_16, edge_attr_4, edge_attr_64, node_vec1)
    x, src, dst, edge_attr_16, edge_attr_4, edge_attr_64, node_vec1 = _rec_inputs()

    def _L0_gnn_setup():
        import jax, jax.numpy as jnp
        import numpy as np
        EPS = 1e-05

        def _sage_conv(h, src, dst, n_nodes, Wl, bl, Wr):
            msg = jnp.take(h, src, axis=0)
            agg = jax.ops.segment_sum(msg, dst, num_segments=n_nodes)
            cnt = jax.ops.segment_sum(jnp.ones_like(src, dtype=h.dtype), dst, num_segments=n_nodes)
            agg = agg / jnp.clip(cnt, 1.0)[:, None]
            return agg @ Wl + bl + h @ Wr

        def _batchnorm(h, gamma, beta):
            mu = jnp.mean(h, axis=0)
            var = jnp.mean((h - mu) ** 2, axis=0)
            return (h - mu) * jax.lax.rsqrt(var + EPS) * gamma + beta
        key = jax.random.key(seed)
        ks = jax.random.split(key, 16)
        N, E, IN, H, OUT = (12500, 100000, 128, 256, 128)
        x = jax.random.normal(ks[0], (N, IN), dtype=jnp.float32)
        edge_index = jax.random.randint(ks[1], (2, E), 0, N, dtype=jnp.int32)

        def lin(k, din, dout):
            s = 1.0 / np.sqrt(din)
            return jax.random.uniform(k, (din, dout), jnp.float32, -s, s)
        return {'x': x, 'edge_index': edge_index, 'Wl0': lin(ks[2], IN, H), 'bl0': jnp.zeros((H,), jnp.float32), 'Wr0': lin(ks[3], IN, H), 'g0': jnp.ones((H,), jnp.float32), 'b0': jnp.zeros((H,), jnp.float32), 'Wl1': lin(ks[4], H, H), 'bl1': jnp.zeros((H,), jnp.float32), 'Wr1': lin(ks[5], H, H), 'g1': jnp.ones((H,), jnp.float32), 'b1': jnp.zeros((H,), jnp.float32), 'Wp': lin(ks[6], H, OUT), 'bp': jnp.zeros((OUT,), jnp.float32)}
    _L0_gnn_all = _L0_gnn_setup()
    _L0_gnn_in = {k: v for k, v in _L0_gnn_all.items() if k in ('Wl0', 'bl0', 'Wr0', 'g0', 'b0', 'Wl1', 'bl1', 'Wr1', 'g1', 'b1', 'Wp', 'bp')}
    del _L0_gnn_all

    def _L1_gnn_setup():
        import jax, jax.numpy as jnp
        import numpy as np
        EPS = 1e-07
        N_NODES, N_EDGES, D = (1250, 20000, 128)

        def mobius_add(x, y):
            x2 = jnp.sum(x * x, axis=-1, keepdims=True)
            y2 = jnp.sum(y * y, axis=-1, keepdims=True)
            xy = jnp.sum(x * y, axis=-1, keepdims=True)
            num = (1.0 + 2.0 * xy + y2) * x + (1.0 - x2) * y
            den = 1.0 + 2.0 * xy + x2 * y2
            return num / jnp.maximum(den, EPS)

        def mobius_scalar_mul(r, x):
            nrm = jnp.sqrt(jnp.sum(x * x, axis=-1, keepdims=True))
            nrm_c = jnp.clip(nrm, EPS, 1.0 - EPS)
            scaled = jnp.tanh(r * jnp.arctanh(nrm_c)) * (x / nrm_c)
            return jnp.where(nrm > EPS, scaled, jnp.zeros_like(x))
        key = jax.random.key(seed)
        kx, ke = jax.random.split(key)
        raw = jax.random.normal(kx, (N_NODES, D), dtype=jnp.float32)
        x = 0.4 * raw / (1.0 + jnp.linalg.norm(raw, axis=-1, keepdims=True))
        edge_index = jax.random.randint(ke, (2, N_EDGES), 0, N_NODES, dtype=jnp.int64)
        return {'x': x, 'edge_index': edge_index}
    _L1_gnn_all = _L1_gnn_setup()
    _L1_gnn_in = {k: v for k, v in _L1_gnn_all.items() if k in ()}
    del _L1_gnn_all

    def _L2_gnn_setup():
        import jax, jax.numpy as jnp
        import numpy as np
        MUL = 32
        N_NODES = 6250
        N_EDGES = 100000
        NUM_NEIGHBORS = 16.0
        SQRT3 = 3.0 ** 0.5
        SILU_NORM = 1.679

        def split_irreps(x):
            x0 = x[..., :MUL]
            x1 = x[..., MUL:].reshape(x.shape[:-1] + (MUL, 3))
            return (x0, x1)

        def merge_irreps(x0, x1):
            return jnp.concatenate([x0, x1.reshape(x1.shape[:-2] + (MUL * 3,))], axis=-1)

        def fctp_scalar(x0, x1, a, W0, W1, fan_in):
            s = a / jnp.sqrt(jnp.asarray(fan_in, x0.dtype))
            o0 = x0 @ W0 * s
            o1 = jnp.einsum('nud,uw->nwd', x1, W1) * s[..., None]
            return (o0, o1)
        key = jax.random.key(seed)
        ks = jax.random.split(key, 17)
        inp = dict(node_input=jax.random.normal(ks[0], (N_NODES, 4 * MUL), jnp.float32), node_attr=jnp.ones((N_NODES, 1), jnp.float32), edge_src=jax.random.randint(ks[1], (N_EDGES,), 0, N_NODES), edge_dst=jax.random.randint(ks[2], (N_EDGES,), 0, N_NODES), edge_attr=jax.random.normal(ks[3], (N_EDGES, 4), jnp.float32), edge_scalars=jax.random.normal(ks[4], (N_EDGES, 64), jnp.float32))
        p = lambda k, sh: jax.random.normal(k, sh, jnp.float32)
        inp.update(W_sc0=p(ks[5], (MUL, MUL)), W_sc1=p(ks[6], (MUL, MUL)), W_l1_0=p(ks[7], (MUL, MUL)), W_l1_1=p(ks[8], (MUL, MUL)), W_fc1=p(ks[9], (64, 64)), W_fc2=p(ks[10], (64, 4 * MUL)), W_l2_A0=p(ks[11], (MUL, MUL)), W_l2_B0=p(ks[12], (MUL, MUL)), W_l2_C1=p(ks[13], (MUL, MUL)), W_l2_D1=p(ks[14], (MUL, MUL)), W_l3_A=p(ks[15], (MUL, 1)), W_l3_B=p(ks[16], (MUL, 1)))
        return inp
    _L2_gnn_all = _L2_gnn_setup()
    _L2_gnn_in = {k: v for k, v in _L2_gnn_all.items() if k in ('W_sc0', 'W_sc1', 'W_l1_0', 'W_l1_1', 'W_fc1', 'W_fc2', 'W_l2_A0', 'W_l2_B0', 'W_l2_C1', 'W_l2_D1', 'W_l3_A', 'W_l3_B')}
    del _L2_gnn_all

    def _L3_gnn_setup():
        import jax, jax.numpy as jnp
        import numpy as np
        N = 6250
        E = 100000
        H = 4
        C = 32
        DIN = 128
        ED = 16
        NEG = 0.2
        EPS = 1e-05
        key = jax.random.key(seed)
        ks = jax.random.split(key, 12)
        s = 0.05
        return {'x': jax.random.normal(ks[0], (N, DIN), dtype=jnp.float32), 'edge_index': jax.random.randint(ks[1], (2, E), 0, N, dtype=jnp.int64), 'edge_attr': jax.random.normal(ks[2], (E, ED), dtype=jnp.float32), 'W_ep': jax.random.normal(ks[3], (ED, ED), dtype=jnp.float32) * s, 'b_ep': jnp.zeros((ED,), dtype=jnp.float32), 'W_lin': jax.random.normal(ks[4], (DIN, H * C), dtype=jnp.float32) * s, 'W_edge': jax.random.normal(ks[5], (ED, H * C), dtype=jnp.float32) * s, 'att_src': jax.random.normal(ks[6], (H, C), dtype=jnp.float32) * s, 'att_dst': jax.random.normal(ks[7], (H, C), dtype=jnp.float32) * s, 'att_edge': jax.random.normal(ks[8], (H, C), dtype=jnp.float32) * s, 'bias': jnp.zeros((H * C,), dtype=jnp.float32), 'ln_g': jnp.ones((H * C,), dtype=jnp.float32), 'ln_b': jnp.zeros((H * C,), dtype=jnp.float32)}
    _L3_gnn_all = _L3_gnn_setup()
    _L3_gnn_in = {k: v for k, v in _L3_gnn_all.items() if k in ('W_ep', 'b_ep', 'W_lin', 'W_edge', 'att_src', 'att_dst', 'att_edge', 'bias', 'ln_g', 'ln_b')}
    del _L3_gnn_all
    return {'x': x, 'src': src, 'dst': dst, 'edge_attr_16': edge_attr_16, 'edge_attr_4': edge_attr_4, 'edge_attr_64': edge_attr_64, 'node_vec1': node_vec1, 'L0_gnn_Wl0': _L0_gnn_in['Wl0'], 'L0_gnn_bl0': _L0_gnn_in['bl0'], 'L0_gnn_Wr0': _L0_gnn_in['Wr0'], 'L0_gnn_g0': _L0_gnn_in['g0'], 'L0_gnn_b0': _L0_gnn_in['b0'], 'L0_gnn_Wl1': _L0_gnn_in['Wl1'], 'L0_gnn_bl1': _L0_gnn_in['bl1'], 'L0_gnn_Wr1': _L0_gnn_in['Wr1'], 'L0_gnn_g1': _L0_gnn_in['g1'], 'L0_gnn_b1': _L0_gnn_in['b1'], 'L0_gnn_Wp': _L0_gnn_in['Wp'], 'L0_gnn_bp': _L0_gnn_in['bp'], 'L2_gnn_W_sc0': _L2_gnn_in['W_sc0'], 'L2_gnn_W_sc1': _L2_gnn_in['W_sc1'], 'L2_gnn_W_l1_0': _L2_gnn_in['W_l1_0'], 'L2_gnn_W_l1_1': _L2_gnn_in['W_l1_1'], 'L2_gnn_W_fc1': _L2_gnn_in['W_fc1'], 'L2_gnn_W_fc2': _L2_gnn_in['W_fc2'], 'L2_gnn_W_l2_A0': _L2_gnn_in['W_l2_A0'], 'L2_gnn_W_l2_B0': _L2_gnn_in['W_l2_B0'], 'L2_gnn_W_l2_C1': _L2_gnn_in['W_l2_C1'], 'L2_gnn_W_l2_D1': _L2_gnn_in['W_l2_D1'], 'L2_gnn_W_l3_A': _L2_gnn_in['W_l3_A'], 'L2_gnn_W_l3_B': _L2_gnn_in['W_l3_B'], 'L3_gnn_W_ep': _L3_gnn_in['W_ep'], 'L3_gnn_b_ep': _L3_gnn_in['b_ep'], 'L3_gnn_W_lin': _L3_gnn_in['W_lin'], 'L3_gnn_W_edge': _L3_gnn_in['W_edge'], 'L3_gnn_att_src': _L3_gnn_in['att_src'], 'L3_gnn_att_dst': _L3_gnn_in['att_dst'], 'L3_gnn_att_edge': _L3_gnn_in['att_edge'], 'L3_gnn_bias': _L3_gnn_in['bias'], 'L3_gnn_ln_g': _L3_gnn_in['ln_g'], 'L3_gnn_ln_b': _L3_gnn_in['ln_b']}

def reference(x, src, dst, edge_attr_16, edge_attr_4, edge_attr_64, node_vec1, L0_gnn_Wl0, L0_gnn_bl0, L0_gnn_Wr0, L0_gnn_g0, L0_gnn_b0, L0_gnn_Wl1, L0_gnn_bl1, L0_gnn_Wr1, L0_gnn_g1, L0_gnn_b1, L0_gnn_Wp, L0_gnn_bp, L2_gnn_W_sc0, L2_gnn_W_sc1, L2_gnn_W_l1_0, L2_gnn_W_l1_1, L2_gnn_W_fc1, L2_gnn_W_fc2, L2_gnn_W_l2_A0, L2_gnn_W_l2_B0, L2_gnn_W_l2_C1, L2_gnn_W_l2_D1, L2_gnn_W_l3_A, L2_gnn_W_l3_B, L3_gnn_W_ep, L3_gnn_b_ep, L3_gnn_W_lin, L3_gnn_W_edge, L3_gnn_att_src, L3_gnn_att_dst, L3_gnn_att_edge, L3_gnn_bias, L3_gnn_ln_g, L3_gnn_ln_b):
    import jax
    import jax.numpy as jnp

    def _L0_gnn_ref(x, edge_index, Wl0, bl0, Wr0, g0, b0, Wl1, bl1, Wr1, g1, b1, Wp, bp):
        import jax, jax.numpy as jnp
        import numpy as np
        EPS = 1e-05

        def _sage_conv(h, src, dst, n_nodes, Wl, bl, Wr):
            msg = jnp.take(h, src, axis=0)
            agg = jax.ops.segment_sum(msg, dst, num_segments=n_nodes)
            cnt = jax.ops.segment_sum(jnp.ones_like(src, dtype=h.dtype), dst, num_segments=n_nodes)
            agg = agg / jnp.clip(cnt, 1.0)[:, None]
            return agg @ Wl + bl + h @ Wr

        def _batchnorm(h, gamma, beta):
            mu = jnp.mean(h, axis=0)
            var = jnp.mean((h - mu) ** 2, axis=0)
            return (h - mu) * jax.lax.rsqrt(var + EPS) * gamma + beta
        src, dst = (edge_index[0], edge_index[1])
        n = x.shape[0]
        h = _sage_conv(x, src, dst, n, Wl0, bl0, Wr0)
        h = _batchnorm(jax.nn.relu(h), g0, b0)
        h = _sage_conv(h, src, dst, n, Wl1, bl1, Wr1)
        h = _batchnorm(jax.nn.relu(h), g1, b1)
        return jax.nn.relu(h @ Wp + bp)

    def _L1_gnn_ref(x, edge_index):
        import jax, jax.numpy as jnp
        import numpy as np
        EPS = 1e-07
        N_NODES, N_EDGES, D = (1250, 20000, 128)

        def mobius_add(x, y):
            x2 = jnp.sum(x * x, axis=-1, keepdims=True)
            y2 = jnp.sum(y * y, axis=-1, keepdims=True)
            xy = jnp.sum(x * y, axis=-1, keepdims=True)
            num = (1.0 + 2.0 * xy + y2) * x + (1.0 - x2) * y
            den = 1.0 + 2.0 * xy + x2 * y2
            return num / jnp.maximum(den, EPS)

        def mobius_scalar_mul(r, x):
            nrm = jnp.sqrt(jnp.sum(x * x, axis=-1, keepdims=True))
            nrm_c = jnp.clip(nrm, EPS, 1.0 - EPS)
            scaled = jnp.tanh(r * jnp.arctanh(nrm_c)) * (x / nrm_c)
            return jnp.where(nrm > EPS, scaled, jnp.zeros_like(x))
        src, dst = (edge_index[0], edge_index[1])
        n, d = x.shape
        messages = mobius_add(x[src], -x[dst])

        def body(out, em):
            m, idx = em
            return (out.at[idx].set(mobius_add(out[idx], m)), None)
        out0 = jnp.zeros((n, d), dtype=x.dtype)
        total, _ = jax.lax.scan(body, out0, (messages, dst))
        count = jnp.zeros((n,), dtype=x.dtype).at[dst].add(1.0)
        scale = 1.0 / jnp.maximum(count, 1.0)
        aggr = mobius_scalar_mul(scale[:, None], total)
        return mobius_add(x, aggr)

    def _L2_gnn_ref(node_input, node_attr, edge_src, edge_dst, edge_attr, edge_scalars, W_sc0, W_sc1, W_l1_0, W_l1_1, W_fc1, W_fc2, W_l2_A0, W_l2_B0, W_l2_C1, W_l2_D1, W_l3_A, W_l3_B):
        import jax, jax.numpy as jnp
        import numpy as np
        MUL = 32
        N_NODES = 6250
        N_EDGES = 100000
        NUM_NEIGHBORS = 16.0
        SQRT3 = 3.0 ** 0.5
        SILU_NORM = 1.679

        def split_irreps(x):
            x0 = x[..., :MUL]
            x1 = x[..., MUL:].reshape(x.shape[:-1] + (MUL, 3))
            return (x0, x1)

        def merge_irreps(x0, x1):
            return jnp.concatenate([x0, x1.reshape(x1.shape[:-2] + (MUL * 3,))], axis=-1)

        def fctp_scalar(x0, x1, a, W0, W1, fan_in):
            s = a / jnp.sqrt(jnp.asarray(fan_in, x0.dtype))
            o0 = x0 @ W0 * s
            o1 = jnp.einsum('nud,uw->nwd', x1, W1) * s[..., None]
            return (o0, o1)
        n = node_input.shape[0]
        x0, x1 = split_irreps(node_input)
        h = SILU_NORM * jax.nn.silu(edge_scalars @ (W_fc1 / 8.0))
        weight = h @ (W_fc2 / 8.0)
        sc0, sc1 = fctp_scalar(x0, x1, node_attr, W_sc0, W_sc1, MUL)
        f0, f1 = fctp_scalar(x0, x1, node_attr, W_l1_0, W_l1_1, MUL)
        g0 = f0[edge_src]
        g1 = f1[edge_src]
        e0 = edge_attr[:, :1]
        e1 = edge_attr[:, 1:]
        wA, wC, wD, wB = (weight[:, :MUL], weight[:, MUL:2 * MUL], weight[:, 2 * MUL:3 * MUL], weight[:, 3 * MUL:])
        outA = wA * g0 * e0
        outB = wB * jnp.einsum('euk,ek->eu', g1, e1) / SQRT3
        outC = (wC * g0)[..., None] * e1[:, None, :]
        outD = wD[..., None] * g1 * e0[..., None]
        seg = lambda v: jax.ops.segment_sum(v, edge_dst, num_segments=n)
        inv = 1.0 / jnp.sqrt(jnp.asarray(NUM_NEIGHBORS, node_input.dtype))
        mA, mB, mC, mD = (seg(outA) * inv, seg(outB) * inv, seg(outC) * inv, seg(outD) * inv)
        s = node_attr / 8.0
        c0 = (mA @ W_l2_A0 + mB @ W_l2_B0) * s
        c1 = (jnp.einsum('nud,uw->nwd', mC, W_l2_C1) + jnp.einsum('nud,uw->nwd', mD, W_l2_D1)) * s[..., None]
        angle = 0.1 * (mA @ W_l3_A + mB @ W_l3_B) * s
        cos, sin = (jnp.cos(angle), jnp.sin(angle))
        return cos * merge_irreps(sc0, sc1) + sin * merge_irreps(c0, c1)

    def _L3_gnn_ref(x, edge_index, edge_attr, W_ep, b_ep, W_lin, W_edge, att_src, att_dst, att_edge, bias, ln_g, ln_b):
        import jax, jax.numpy as jnp
        import numpy as np
        N = 6250
        E = 100000
        H = 4
        C = 32
        DIN = 128
        ED = 16
        NEG = 0.2
        EPS = 1e-05
        n = x.shape[0]
        src, dst = (edge_index[0], edge_index[1])
        ea = jax.nn.relu(edge_attr @ W_ep + b_ep)
        ones = jnp.ones((ea.shape[0],), dtype=ea.dtype)
        deg = jax.ops.segment_sum(ones, dst, num_segments=n)
        loop_attr = jax.ops.segment_sum(ea, dst, num_segments=n)
        loop_attr = loop_attr / jnp.maximum(deg, 1.0)[:, None]
        loop = jnp.arange(n, dtype=src.dtype)
        src2 = jnp.concatenate([src, loop])
        dst2 = jnp.concatenate([dst, loop])
        ea2 = jnp.concatenate([ea, loop_attr], axis=0)
        h = (x @ W_lin).reshape(n, H, C)
        a_src = jnp.einsum('nhc,hc->nh', h, att_src)
        a_dst = jnp.einsum('nhc,hc->nh', h, att_dst)
        e = (ea2 @ W_edge).reshape(-1, H, C)
        a_e = jnp.einsum('ehc,hc->eh', e, att_edge)
        alpha = a_src[src2] + a_dst[dst2] + a_e
        alpha = jnp.where(alpha >= 0, alpha, NEG * alpha)
        m = jax.ops.segment_max(alpha, dst2, num_segments=n)
        ex = jnp.exp(alpha - m[dst2])
        denom = jax.ops.segment_sum(ex, dst2, num_segments=n)
        w = ex / denom[dst2]
        msg = h[src2] * w[:, :, None]
        out = jax.ops.segment_sum(msg, dst2, num_segments=n)
        out = out.reshape(n, H * C) + bias
        out = out + x
        mu = jnp.mean(out, axis=-1, keepdims=True)
        var = jnp.var(out, axis=-1, keepdims=True)
        out = (out - mu) * jax.lax.rsqrt(var + EPS) * ln_g + ln_b
        return out
    edge_index = jnp.stack([src, dst])
    x = _layernorm(x + _L0_gnn_ref(x, edge_index, L0_gnn_Wl0, L0_gnn_bl0, L0_gnn_Wr0, L0_gnn_g0, L0_gnn_b0, L0_gnn_Wl1, L0_gnn_bl1, L0_gnn_Wr1, L0_gnn_g1, L0_gnn_b1, L0_gnn_Wp, L0_gnn_bp), axis=-1)
    x = _layernorm(x + _L1_gnn_ref(x, edge_index), axis=-1)
    x = _layernorm(x + _L2_gnn_ref(x, node_vec1, src, dst, edge_attr_4, edge_attr_64, L2_gnn_W_sc0, L2_gnn_W_sc1, L2_gnn_W_l1_0, L2_gnn_W_l1_1, L2_gnn_W_fc1, L2_gnn_W_fc2, L2_gnn_W_l2_A0, L2_gnn_W_l2_B0, L2_gnn_W_l2_C1, L2_gnn_W_l2_D1, L2_gnn_W_l3_A, L2_gnn_W_l3_B), axis=-1)
    x = _layernorm(x + _L3_gnn_ref(x, edge_index, edge_attr_16, L3_gnn_W_ep, L3_gnn_b_ep, L3_gnn_W_lin, L3_gnn_W_edge, L3_gnn_att_src, L3_gnn_att_dst, L3_gnn_att_edge, L3_gnn_bias, L3_gnn_ln_g, L3_gnn_ln_b), axis=-1)
    return x

_drawn_inputs = setup_inputs


def setup_inputs(seed=0):
    import zlib

    import numpy as np

    out = dict(_drawn_inputs(seed))
    spreads = {'L0_gnn_bl0': (0.0, 0.1),
     'L0_gnn_g0': (1.0, 0.2),
     'L0_gnn_b0': (0.0, 0.1),
     'L0_gnn_bl1': (0.0, 0.1),
     'L0_gnn_g1': (1.0, 0.2),
     'L0_gnn_b1': (0.0, 0.1),
     'L0_gnn_bp': (0.0, 0.1),
     'L3_gnn_b_ep': (0.0, 0.8),
     'L3_gnn_bias': (0.0, 0.1),
     'L3_gnn_ln_g': (1.0, 0.2),
     'L3_gnn_ln_b': (0.0, 0.1)}
    factors = {'edge_attr_16': 8.0,
     'edge_attr_4': 4.916,
     'edge_attr_64': 4.931,
     'L2_gnn_W_l1_0': 5.901,
     'L2_gnn_W_l1_1': 5.3,
     'L2_gnn_W_fc1': 4.904,
     'L2_gnn_W_fc2': 4.824,
     'L2_gnn_W_l2_A0': 8.0,
     'L2_gnn_W_l2_B0': 8.0,
     'L2_gnn_W_l2_C1': 7.601,
     'L2_gnn_W_l2_D1': 7.747,
     'L2_gnn_W_l3_A': 7.223,
     'L2_gnn_W_l3_B': 5.293,
     'L3_gnn_W_ep': 8.0,
     'L3_gnn_W_edge': 8.0,
     'L3_gnn_att_src': 5.147,
     'L3_gnn_att_dst': 64.0,
     'L3_gnn_att_edge': 8.0,
     'L2_gnn_W_sc0': 36.021,
     'L2_gnn_W_sc1': 21.558}
    for name, (base, spread) in spreads.items():
        noise = np.random.default_rng([zlib.crc32(name.encode()), seed]).standard_normal(out[name].shape)
        drawn = base * np.exp(spread * noise) if base else spread * noise
        out[name] = jnp.asarray(drawn.astype(out[name].dtype))
    for name, factor in factors.items():
        out[name] = (out[name] * factor).astype(out[name].dtype)
    return out
```

```python
from contextlib import ExitStack

import numpy as np

import concourse.bass as bass
from concourse import mybir

F32 = mybir.dt.float32
I32 = mybir.dt.int32
BF16 = mybir.dt.bfloat16
ALU = mybir.AluOpType
ACT = mybir.ActivationFunctionType
AX_X = mybir.AxisListType.X

P = 128
N = 6250
E = 106250
D = 128
TILES = -(-N // P)
NP = TILES * P
ETILES = -(-E // P)
U = 8
BODIES = -(-(ETILES + TILES) // U)
STEPS = BODIES * U
EROWS = 7 * P
EP = EROWS * P
DST_PAD = 8191
HID = 256
CH = 448
NCH = NP // CH
EB = 1024
EBP = BODIES * EB
RUN = 32
RUNS = EBP // RUN
EF = 5
G = 7
GROUPS = TILES // G
R = 4
CBODY = RUN // R
MAXB = E // R + 2
XW = 132
HW = 136
BIG = 1.0e30
WB = U // 2
WTILES = 2 * BODIES * WB
WW = D + 4
SILU_NORM = 1.679


class Semaphores:

    def __init__(self, nc, ctx, prefix=""):
        self.nc, self.prefix, self.taken = nc, prefix, []
        ctx.callback(self.clear)

    def clear(self):
        self.nc.clear_and_free_semaphores(self.taken)
        self.nc.all_engine_barrier(sem_only=True)

    def __call__(self, name):
        self.taken.append(self.nc.alloc_semaphore(self.prefix + name))
        return self.taken[-1]


class Chain:

    def __init__(self, eng, sem, base=0, took=None):
        self.eng, self.sem, self.base, self.n, self.took = eng, sem, base, 0, took

    def put(self, ins):
        ins.then_inc(self.sem, 1)
        self.n += 1

    def sync(self):
        self.eng.wait_ge(self.sem, self.base + self.n)
        if self.took is not None:
            self.eng.sem_inc(self.took, 1)

    def __call__(self, ins):
        self.put(ins)
        self.sync()


def build(nc, a, out):
    ctx = ExitStack()

    def dram(name, shape, dt=F32):
        return nc.dram_tensor(name, shape, dt).ap()

    with ctx:
        def sb(name, shape, dt=F32, where=ctx):
            return where.enter_context(nc.sbuf_tensor(name, shape, dt))

        t = {
            "ptr": dram("ptr_tab", (NP + P,), I32),
            "rc": dram("rc_tab", (NP,)),
            "stepT": dram("step_node_tile", (EROWS,), I32),
            "stepE": dram("step_edge_tile", (EROWS,), I32),
            "srt": dram("sorted_nodes", (NP, 4), I32),
            "edge": dram("edge_tab", (RUNS, RUN * EF)),
            "w": dram("w_tab", (WTILES * P, WW)),
            "x3": dram("x3_tab", (NP, D)),
            "xs": dram("x_split", (NP, 3 * D), BF16),
            "ys": dram("y_split", (NP, 3 * HID), BF16),
            "x1": dram("x1_tab", (NP, XW)),
            "x2": dram("x2_tab", (NP, D)),
            "f": dram("f_tab", (NP, D)),
            "h": dram("h_tab", (NP, HW)),
            "hx": dram("hx_tab", (NP, HW + D)),
        }
        s = {
            "srcS": sb("srcS", [P, EROWS], I32),
            "dstS": sb("dstS", [P, EROWS]),
            "iota": sb("iota", [P, P]),
            "ident": sb("ident", [P, P]),
            "ones": sb("ones", [P, P]),
            "part": sb("part", [P, 1]),
            "eighth": sb("eighth", [P, 8]),
            "stepE": sb("stepE", [1, EROWS], I32),
            "stepT": sb("stepT", [1, EROWS // 4], I32),
            "perm": sb("perm", [P, TILES], I32),
            "sdeg": sb("sdeg", [P, TILES]),
            "srow": sb("srow", [P, TILES]),
            "sbit": sb("sbit", [P, 5, TILES], I32),
            "rounds": sb("rounds", [1, 4, GROUPS], I32),
        }
        setup(nc, a, t, s)
        sage(nc, a, t, s)
        moebius(nc, a, t, s)
        equivariant(nc, a, t, s)
        gat(nc, a, t, s, out)
    return nc


def broadcast(ap, shape, axis):
    return ap.unsqueeze(axis).broadcast_to(shape)


def node_tiles(eng, s, i4):
    word = eng.value_load(s["stepT"][0:1, bass.ds(i4, 1)], min_val=0, max_val=(1 << 24) - 1)
    return [eng.snap((word >> (6 * n)) & 63).with_bounds(min_val=0, max_val=TILES - 1) for n in range(4)]


def setup(nc, a, t, s):
    with ExitStack() as ctx:
        def sb(name, shape, dt=F32):
            return ctx.enter_context(nc.sbuf_tensor(name, shape, dt))

        sem = Semaphores(nc, ctx)
        rows_i = sb("rows_i", [P, 7, P], I32)
        rows_f = sb("rows_f", [P, 7, P])
        srow_i = sb("srow_i", [P, 2, 7, P], I32)
        srow_f = sb("srow_f", [P, 2, 7, P])
        first_row = sb("first_row", [1, EROWS])
        stepT_i = sb("stepT_i", [1, EROWS], I32)
        pack = sb("pack", [1, 2, EROWS // 4])
        firsts = sb("firsts", [P, ETILES + 1])
        junk = sb("junk", [P, ETILES + 1])
        node_i = sb("node_i", [P, TILES], I32)
        node_f = sb("node_f", [P, TILES])
        iota_i = sb("iota_i", [P, P], I32)
        part_i = sb("part_i", [P, 1], I32)
        part_f = s["part"]
        part8_i = sb("part8_i", [P, 1], I32)
        part8 = sb("part8", [P, 1])
        xin = sb("xin", [P, TILES, D])
        rest = sb("rest", [P, TILES, D])
        xs = sb("xs", [P, TILES, 3, D], BF16)
        step_i = sb("step_i", [P, 7], I32)
        step_f = sb("step_f", [P, 7])
        cnt = sb("cnt", [P, TILES])
        blk = sb("blk", [P, TILES])
        blk_i = sb("blk_i", [P, TILES], I32)
        drow = sb("drow", [P, TILES, P], I32)
        ptr = sb("ptr", [P, TILES])
        ptr_i = sb("ptr_i", [P, TILES], I32)
        last_i = sb("last_i", [1, P], I32)
        nxt_i = sb("nxt_i", [P, TILES], I32)
        deg = sb("deg", [P, TILES])
        rc = sb("rc", [P, TILES])
        bnd_i = sb("bnd_i", [1, TILES], I32)
        bnd = sb("bnd", [1, TILES])
        bndb = sb("bndb", [P, TILES])
        cmpb = sb("cmpb", [P, 7, TILES - 1])
        stT = sb("stT", [P, 7])
        stE = sb("stE", [P, 7])
        st_i = sb("st_i", [P, 2, 7], I32)
        key = sb("key", [P, TILES])
        oh = rest
        cum = sb("cum", [P, TILES + 1, P])
        tri = sb("tri", [P, P])
        tot = sb("tot", [1, P])
        inc = sb("inc", [1, P])
        start = sb("start", [1, P])
        rank = sb("rank", [P, TILES])
        rank_i = sb("rank_i", [P, TILES], I32)
        sval = sb("sval", [P, TILES, 4], I32)
        sback = sb("sback", [P, TILES, 4], I32)
        srow_s = sb("srow_s", [P, TILES], I32)
        dmax = sb("dmax", [P, TILES])
        grow = sb("grow", [1, 6, GROUPS])
        grow_i = sb("grow_i", [1, 2, GROUPS], I32)
        psT = ctx.enter_context(nc.psum_tensor("psT", [P, 4, 512], F32))
        psR = ctx.enter_context(nc.psum_tensor("psR", [P, 2, 512], F32))
        psH = ctx.enter_context(nc.psum_tensor("psH", [P, 512], F32))

        ids_in = sem("ids_in")
        x_in = sem("x_in")
        xs_ready = sem("xs_ready")
        xs_out = sem("xs_out")
        srow_in = sem("srow_in")
        srow_ready = sem("srow_ready")
        iotas = sem("iotas")
        rows_ready = sem("rows_ready")
        turned = sem("turned")
        own = sem("setup_dve")
        firsts_ready = sem("firsts_ready")
        first_spread = sem("first_spread")
        blk_ready = sem("blk_ready")
        drow_in = sem("drow_in")
        ptr_ready = sem("ptr_ready")
        ptr_out = sem("ptr_out")
        nxt_in = sem("nxt_in")
        rc_ready = sem("rc_ready")
        rc_out = sem("rc_out")
        bnd_ready = sem("bnd_ready")
        bnd_spread = sem("bnd_spread")
        steps_ready = sem("steps_ready")
        steps_out = sem("steps_out")
        steps_in = sem("steps_in")
        oh_ready = sem("oh_ready")
        hist_ready = sem("hist_ready")
        start_ready = sem("start_ready")
        place_ready = sem("place_ready")
        place_free = sem("place_free")
        rank_ready = sem("rank_ready")
        scattered = sem("scattered")
        sorted_in = sem("sorted_in")
        deg_ready = sem("deg_ready")
        dmax_ready = sem("dmax_ready")
        block = ctx.enter_context(nc.Block())

        @block.sync
        def _(sp):
            sp.dma_start(rows_i[:], a["dst"].rearrange("(c p k) -> p c k", p=P, k=P)).then_inc(ids_in, 16)
            sp.dma_start(xin[:], a["x"].rearrange("(t p) d -> p t d", p=P)).then_inc(x_in, 16)
            sp.wait_ge(ptr_ready, 1)
            sp.dma_start(t["ptr"][0:NP].rearrange("(t p o) -> p t o", p=P, o=1),
                         ptr_i[:].unsqueeze(2), allow_slow_non_contiguous=True).then_inc(ptr_out, 16)
            sp.dma_start(t["ptr"][NP:NP + P].rearrange("(o p) -> o p", o=1), last_i[:]).then_inc(ptr_out, 16)
            sp.wait_ge(ptr_out, 32)
            sp.dma_start(nxt_i[:].unsqueeze(2),
                         t["ptr"][1:NP + 1].rearrange("(t p o) -> p t o", p=P, o=1),
                         allow_slow_non_contiguous=True).then_inc(nxt_in, 16)
            sp.dma_start(bnd_i[:].unsqueeze(2),
                         t["ptr"][0:NP].rearrange("(o t p) -> o t p", o=1, p=P)[:, :, 0:1],
                         allow_slow_non_contiguous=True).then_inc(nxt_in, 16)
            sp.wait_ge(xs_ready, 1)
            sp.dma_start(t["xs"].rearrange("(t p) d -> p t d", p=P), xs[:].rearrange("p t s d -> p t (s d)")).then_inc(xs_out, 16)
            sp.wait_ge(rc_ready, 1)
            sp.dma_start(t["rc"].rearrange("(t p o) -> p t o", p=P, o=1), rc[:].unsqueeze(2),
                         allow_slow_non_contiguous=True).then_inc(rc_out, 16)
            sp.wait_ge(steps_ready, 1)
            for n, name in enumerate(("stepT", "stepE")):
                sp.dma_start(t[name].rearrange("(c p o) -> p c o", p=P, o=1),
                             st_i[:, n].unsqueeze(2), allow_slow_non_contiguous=True).then_inc(steps_out, 16)
            sp.wait_ge(steps_out, 32)
            sp.dma_start(stepT_i[:], t["stepT"].rearrange("(o n) -> o n", o=1)).then_inc(steps_in, 16)
            sp.dma_start(s["stepE"][:], t["stepE"].rearrange("(o n) -> o n", o=1)).then_inc(steps_in, 16)
            sp.wait_ge(scattered, 16 * TILES)
            sp.dma_start(sback[:], t["srt"].rearrange("(t p) f -> p t f", p=P)).then_inc(sorted_in, 16)
            sp.wait_ge(rc_out, 16)
            sp.wait_ge(xs_out, 16)
            sp.wait_ge(steps_in, 32)

        @block.gpsimd
        def _(pool):
            pool.iota(node_i[:], pattern=[[P, TILES]], base=0, channel_multiplier=1).then_inc(iotas, 1)
            pool.iota(iota_i[:], pattern=[[1, P]], base=0, channel_multiplier=0).then_inc(iotas, 1)
            pool.iota(part_i[:], pattern=[[0, 1]], base=0, channel_multiplier=1).then_inc(iotas, 1)
            pool.iota(step_i[:], pattern=[[P, 7]], base=0, channel_multiplier=1).then_inc(iotas, 1)
            pool.memset(last_i[:], E).then_inc(iotas, 1)
            pool.wait_ge(firsts_ready, 1)
            pool.partition_broadcast(firsts[:], first_row[:, 0:ETILES + 1]).then_inc(first_spread, 1)
            pool.wait_ge(blk_ready, 1)
            for i in range(TILES):
                pool.indirect_dma_start(drow[:, i, :], None, a["dst"].rearrange("(e k) -> e k", k=P),
                                        bass.IndirectOffsetOnAxis(ap=blk_i[:, i:i + 1], axis=0)).then_inc(drow_in, 16)
            pool.wait_ge(bnd_ready, 1)
            pool.partition_broadcast(bndb[:], bnd[:]).then_inc(bnd_spread, 1)
            pool.wait_ge(steps_ready, 1)
            for n, name in enumerate(("src", "dst")):
                for c in range(7):
                    pool.indirect_dma_start(srow_i[:, n, c, :], None, a[name].rearrange("(e k) -> e k", k=P),
                                            bass.IndirectOffsetOnAxis(ap=st_i[:, 1, c:c + 1], axis=0)).then_inc(srow_in, 16)
            pool.wait_ge(rank_ready, 1)
            for i in range(TILES):
                pool.indirect_dma_start(t["srt"][:, :], bass.IndirectOffsetOnAxis(ap=rank_i[:, i:i + 1], axis=0),
                                        sval[:, i, :], None).then_inc(scattered, 16)
            pool.wait_ge(deg_ready, 1)
            pool.partition_all_reduce(dmax[:], s["sdeg"][:], P, bass.bass_isa.ReduceOp.max).then_inc(dmax_ready, 1)

        @block.tensor
        def _(pe):
            pe.wait_ge(rows_ready, 2)
            for c in range(7):
                last = pe.transpose(psT[:, c // 4, (c % 4) * P:(c % 4 + 1) * P], rows_f[:, c], s["ident"][:])
            last.then_inc(turned, 1)
            pe.wait_ge(srow_ready, 1)
            for n in range(2):
                for c in range(7):
                    last = pe.transpose(psT[:, 2 * n + c // 4, (c % 4) * P:(c % 4 + 1) * P], srow_f[:, n, c], s["ident"][:])
            last.then_inc(turned, 1)
            pe.wait_ge(oh_ready, 2)
            pe.matmul(psH[0:1, 0:P], s["ones"][:, 0:1], cum[:, TILES, :], start=True, stop=True).then_inc(hist_ready, 1)
            pe.wait_ge(start_ready, 1)
            for i in range(TILES):
                if i >= 2:
                    pe.wait_ge(place_free, i - 1)
                pe.matmul(psR[:, i % 2, 0:P], s["ones"][:], cum[:, i, :], start=True, stop=False)
                pe.matmul(psR[:, i % 2, 0:P], tri[:], oh[:, i, :], start=False, stop=False)
                pe.matmul(psR[:, i % 2, 0:P], s["ones"][0:1, :], start[:], start=False, stop=True).then_inc(place_ready, 1)

        @block.vector
        def _(dve):
            do = Chain(dve, own)
            dve.wait_ge(iotas, 5)
            do.put(dve.memset(s["ones"][:], 1.0))
            do.put(dve.memset(cum[:, 0, :], 0.0))
            do.put(dve.memset(inc[:], 1.0))
            do.put(dve.tensor_copy(node_f[:], node_i[:]))
            do.put(dve.tensor_copy(s["iota"][:], iota_i[:]))
            do.put(dve.tensor_copy(part_f[:], part_i[:]))
            do(dve.tensor_copy(step_f[:], step_i[:]))
            do.put(dve.tensor_scalar(tri[:], s["iota"][:], part_f[:], None, ALU.is_gt))
            do(dve.tensor_scalar(part8_i[:], part_i[:], 4, None, ALU.logical_shift_right))
            do(dve.tensor_copy(part8[:], part8_i[:]))
            do.put(dve.tensor_scalar(s["eighth"][:], s["iota"][:, 0:8], part8[:], None, ALU.is_equal))
            do.put(dve.tensor_scalar(s["ident"][:], s["iota"][:], part_f[:], None, ALU.is_equal))
            dve.wait_ge(ids_in, 16)
            do.sync()
            dve.tensor_copy(rows_f[:], rows_i[:]).then_inc(rows_ready, 2)
            dve.wait_ge(turned, 1)
            for lo, hi, b in ((0, 512, 0), (512, EROWS, 1)):
                do(dve.tensor_copy(first_row[:, lo:hi], psT[0:1, b, 0:hi - lo]))
            dve.sem_inc(firsts_ready, 1)
            dve.wait_ge(first_spread, 1)
            for i in range(TILES):
                do(dve.tensor_scalar(junk[:], firsts[:], node_f[:, i:i + 1], 0.0, ALU.is_lt, ALU.add,
                                     accum_out=cnt[:, i:i + 1]))
            do(dve.tensor_scalar(blk[:], cnt[:], -1.0, 0.0, ALU.add, ALU.max))
            do(dve.tensor_copy(blk_i[:], blk[:]))
            dve.sem_inc(blk_ready, 1)
            dve.wait_ge(x_in, 16)
            do(dve.tensor_copy(xs[:, :, 0], xin[:]))
            do(dve.tensor_tensor(rest[:], xin[:], xs[:, :, 0], ALU.subtract))
            do(dve.tensor_copy(xs[:, :, 1], rest[:]))
            do(dve.tensor_tensor(xs[:, :, 2], rest[:], xs[:, :, 1], ALU.subtract))
            dve.sem_inc(xs_ready, 1)
            dve.wait_ge(drow_in, 16 * TILES)
            for i in range(TILES):
                do(dve.tensor_scalar(junk[:, 0:P], drow[:, i, :], node_f[:, i:i + 1], 0.0, ALU.is_lt, ALU.add,
                                     accum_out=cnt[:, i:i + 1]))
            do(dve.scalar_tensor_tensor(ptr[:], blk[:], float(P), cnt[:], ALU.mult, ALU.add))
            do(dve.tensor_copy(ptr_i[:], ptr[:]))
            dve.sem_inc(ptr_ready, 1)
            dve.wait_ge(nxt_in, 32)
            do.put(dve.tensor_tensor(deg[:], nxt_i[:], ptr[:], ALU.subtract))
            do(dve.tensor_scalar(bnd_i[:], bnd_i[:], 7, None, ALU.logical_shift_right))
            do.put(dve.tensor_scalar(rc[:], deg[:], 1.0, None, ALU.max))
            do(dve.tensor_tensor(bnd[:], bnd_i[:], s["iota"][0:1, 0:TILES], ALU.add))
            dve.sem_inc(bnd_ready, 1)
            do(dve.reciprocal(rc[:], rc[:]))
            dve.sem_inc(rc_ready, 1)
            dve.wait_ge(bnd_spread, 1)
            do(dve.tensor_tensor(cmpb[:], step_f[:].unsqueeze(2).broadcast_to([P, 7, TILES - 1]),
                                 bndb[:, 1:TILES].unsqueeze(1).broadcast_to([P, 7, TILES - 1]), ALU.is_ge))
            do(dve.tensor_reduce(stT[:], cmpb[:], AX_X, ALU.add))
            do(dve.tensor_tensor(stE[:], step_f[:], stT[:], ALU.subtract))
            do.put(dve.tensor_copy(st_i[:, 0], stT[:]))
            do(dve.tensor_copy(st_i[:, 1], stE[:]))
            dve.sem_inc(steps_ready, 1)
            dve.wait_ge(srow_in, 16 * 14)
            do(dve.tensor_scalar(stT[:], stT[:], float(P), None, ALU.mult))
            do.put(dve.tensor_copy(srow_f[:, 0], srow_i[:, 0]))
            do(dve.tensor_tensor(srow_f[:, 1], srow_i[:, 1], broadcast(stT[:], [P, 7, P], 2), ALU.subtract))
            dve.sem_inc(srow_ready, 1)
            dve.wait_ge(turned, 2)
            for lo, hi, b in ((0, 512, 0), (512, EROWS, 1)):
                do.put(dve.tensor_copy(s["srcS"][:, lo:hi], psT[:, b, 0:hi - lo]))
                do.put(dve.tensor_copy(s["dstS"][:, lo:hi], psT[:, 2 + b, 0:hi - lo]))
            dve.wait_ge(steps_in, 32)
            four = stepT_i[:].rearrange("o (n f) -> o n f", f=4)
            do(dve.tensor_copy(pack[:, 1], four[:, :, 3]))
            for f in (2, 1, 0):
                do(dve.scalar_tensor_tensor(pack[:, f % 2], pack[:, (f + 1) % 2], 64.0, four[:, :, f], ALU.mult, ALU.add))
            do(dve.tensor_copy(s["stepT"][:], pack[:, 0]))
            do(dve.tensor_scalar(key[:], deg[:], float(P - 1), -1.0, ALU.min, ALU.mult))
            do(dve.tensor_scalar(key[:], key[:], float(P - 1), None, ALU.add))
            for i in range(TILES):
                do(dve.tensor_scalar(oh[:, i, :], s["iota"][:], key[:, i:i + 1], None, ALU.is_equal))
                do(dve.tensor_tensor(cum[:, i + 1, :], cum[:, i, :], oh[:, i, :], ALU.add))
            dve.sem_inc(oh_ready, 2)
            dve.wait_ge(hist_ready, 1)
            do(dve.tensor_copy(tot[:], psH[0:1, 0:P]))
            do(dve.tensor_tensor_scan(start[:], inc[:], tot[:], 0.0, ALU.mult, ALU.add))
            do(dve.tensor_tensor(start[:], start[:], tot[:], ALU.subtract))
            dve.sem_inc(start_ready, 1)
            for i in range(TILES):
                dve.wait_ge(place_ready, i + 1)
                do(dve.tensor_tensor(junk[:, 0:P], psR[:, i % 2, 0:P], oh[:, i, :], ALU.mult))
                dve.sem_inc(place_free, 1)
                do(dve.tensor_reduce(rank[:, i:i + 1], junk[:, 0:P], AX_X, ALU.add))
            do.put(dve.tensor_copy(rank_i[:], rank[:]))
            do.put(dve.tensor_copy(sval[:, :, 0], node_i[:]))
            do.put(dve.tensor_copy(sval[:, :, 1], ptr_i[:]))
            do.put(dve.tensor_copy(sval[:, :, 2], deg[:]))
            do(dve.memset(sval[:, :, 3], 0))
            dve.sem_inc(rank_ready, 1)
            dve.wait_ge(sorted_in, 16)
            do.put(dve.tensor_copy(s["perm"][:], sback[:, :, 0]))
            do(dve.tensor_scalar(srow_s[:], sback[:, :, 1], 5, None, ALU.logical_shift_right))
            do.put(dve.tensor_copy(s["srow"][:], srow_s[:]))
            for b in range(5):
                do.put(dve.tensor_scalar(s["sbit"][:, b], sback[:, :, 1], 1 << b, None, ALU.bitwise_and))
            do(dve.tensor_copy(s["sdeg"][:], sback[:, :, 2]))
            dve.sem_inc(deg_ready, 1)
            dve.wait_ge(dmax_ready, 1)
            do(dve.tensor_reduce(grow[:, 0], dmax[0:1, :].rearrange("o (g t) -> o g t", t=G), AX_X, ALU.max))
            for n, (add, shift) in enumerate(((R - 1, 2), (R * CBODY - 1, 5))):
                do(dve.tensor_scalar(grow[:, 1], grow[:, 0], float(add), None, ALU.add))
                do(dve.tensor_copy(grow_i[:, 0], grow[:, 1]))
                do(dve.tensor_scalar(grow_i[:, 1], grow_i[:, 0], shift, None, ALU.logical_shift_right))
                do(dve.tensor_copy(grow[:, 2], grow_i[:, 1]))
                do(dve.tensor_tensor_scan(grow[:, 3], inc[0:1, 0:GROUPS], grow[:, 2], 0.0, ALU.mult, ALU.add))
                do(dve.tensor_tensor(grow[:, 4], grow[:, 3], grow[:, 2], ALU.subtract))
                do.put(dve.tensor_copy(s["rounds"][:, 2 * n], grow[:, 2]))
                do(dve.tensor_copy(s["rounds"][:, 2 * n + 1], grow[:, 4]))


class LayerNorm:

    def __init__(self, ctx, nc, new_sem, name):
        sb = lambda n, shape: ctx.enter_context(nc.sbuf_tensor(f"{name}_ln_{n}", shape, F32))
        sem = lambda n: new_sem(f"ln_{n}")
        self.stats, self.mv = sb("stats", [P, G, 6]), sb("mv", [P, G, 2])
        self.var, self.std, self.junk = sb("var", [P, G]), sb("std", [P, G]), sb("junk", [P, D])
        self.own, self.var_ready, self.std_ready = sem("own"), sem("var_ready"), sem("std_ready")
        self.free, self.ready, self.took = sem("free"), sem("ready"), sem("took")

    def scalar(self, act):
        with act.Fori(0, GROUPS) as g:
            act.wait_ge(self.var_ready, g + 1)
            act.activation(self.std[:], self.var[:], ACT.Sqrt).then_inc(self.std_ready, 1)

    def vector(self, dve, v, out, sumsq=False):
        per_group = 3 * G + 1 + G * sumsq
        with dve.Fori(0, GROUPS) as g:
            do = Chain(dve, self.own, g * per_group)
            rows = [v[:, bass.ds(g * G + u, 1)].rearrange("p o d -> p (o d)") for u in range(G)]
            for u in range(G):
                do.put(dve.bn_stats(self.stats[:, u], rows[u]))
            do.sync()
            dve.sem_inc(self.took, 1)
            for u in range(G):
                do.put(dve.bn_aggr(self.mv[:, u], self.stats[:, u]))
            do.sync()
            dve.tensor_scalar(self.var[:], self.mv[:, :, 1], 1e-5, None, ALU.add).then_inc(self.var_ready, 1)
            dve.wait_ge(self.std_ready, g + 1)
            do(dve.reciprocal(self.var[:], self.std[:]))
            dve.wait_ge(self.free, g + 1)
            for u in range(G):
                do.put(dve.tensor_scalar(out(g, u)[:, 0:D], rows[u], self.mv[:, u, 0:1], self.var[:, u:u + 1],
                                         ALU.subtract, ALU.mult))
            if sumsq:
                do.sync()
                for u in range(G):
                    do(dve.tensor_tensor_reduce(out=self.junk[:], in0=out(g, u)[:, 0:D], in1=out(g, u)[:, 0:D],
                                                scale=1.0, scalar=0.0, op0=ALU.mult, op1=ALU.add,
                                                accum_out=out(g, u)[:, D:D + 1]))
            else:
                do.sync()
            dve.sem_inc(self.ready, 1)
            assert do.n == per_group


def sage(nc, a, t, s):
    with ExitStack() as ctx:
        yT = ctx.enter_context(nc.sbuf_tensor("yT", [P, 2, NP], F32))
        rcb = ctx.enter_context(nc.sbuf_tensor("rcb", [P, NP], F32))
        sage_layer(nc, a, t, s, yT, rcb, 0)
        sage_layer(nc, a, t, s, yT, rcb, 1)


def sage_layer(nc, a, t, s, yT, rcb, layer):
    W = (D, HID)[layer]
    KB = W // P
    with ExitStack() as ctx:
        def sb(name, shape, dt=F32):
            return ctx.enter_context(nc.sbuf_tensor(f"{name}{layer}", shape, dt))

        sem = Semaphores(nc, ctx, f"sage{layer}_")
        ps = ctx.enter_context(nc.psum_tensor(f"ps{layer}", [P, 8, 512], F32))
        agg = sb("agg", [P, KB, NP])
        idx = sb("idx", [P, 2, U], I32)
        rows = sb("rows", [P, U, 3 * W], BF16)
        onehot = sb("onehot", [P, U, P], BF16)
        es = sb("es", [P, 2, 2 * P])
        w1d = sb("w1d", [P, P])
        w2d = sb("w2d", [P, 2 * P])
        hT = sb("hT", [P, 2 * P])
        wrow = sb("wrow", [P, 2, WB, WW])
        wl = sb("wl", [P, KB, HID])
        wr = sb("wr", [P, KB, HID])
        vecs = sb("vecs", [P, 3, 2])
        stats = sb("stats", [P, 2, NCH, 6])
        mv = sb("mv", [P, 2, 2])
        scale = sb("scale", [P, 2])
        shift = sb("shift", [P, 2])
        if layer == 0:
            xT = sb("xT", [P, NP])
            ea = sb("ea", [P, 2, P])
            eh = sb("eh", [P, P])
            esrc = sb("esrc", [P, 2, EB // P], I32)
            erow = sb("erow", [P, 2, EB // P, EF])
            wep1 = sb("wep1", [P, 16])
            wep = sb("wep", [P, 8, 16])
            bep = sb("bep", [P, 1])
            wedge = sb("wedge", [P, D])
            atte = sb("atte", [P, D])
            wa1 = sb("wa1", [P, 4])
            wa = sb("wa", [P, 8, 4])
            ystage = sb("ystage", [P, G, 3, HID], BF16)
            yrest = sb("yrest", [P, 2, HID])
            own = xT[:].unsqueeze(1)
        else:
            wp = sb("wp", [P, 2, D])
            bp = sb("bp", [1, D])
            xin = sb("xin", [P, G, D])
            v = yT[:, 0].rearrange("p (t d) -> p t d", d=D)
            ln = LayerNorm(ctx, nc, sem, "sage")
            x1 = sb("x1row", [P, G, XW])
            own = yT

        setup_in = sem("sage_in")
        pool_go = sem("pool_go")
        idx_ready = sem("idx_ready")
        gathered = [sem(f"gathered{u}_") for u in range(U)]
        onehot_ready = sem("onehot_ready")
        step_done = sem("step_done")
        added = sem("added")
        agg_zero = sem("agg_zero")
        agg_ready = sem("agg_ready")
        dense_ready = sem("dense_ready")
        dense_free = sem("dense_free")
        stats_own = sem("stats_own")
        var_ready = sem("var_ready")
        std_ready = sem("std_ready")
        y_ready = sem("y_ready")
        hi_ready = sem("hi_ready")
        rest_ready = sem("rest_ready")
        mid_ready = sem("mid_ready")
        turned = sem("turned")
        staged = sem("staged")
        stored = [sem(f"stored{u}_") for u in range(G)]
        x_in = [sem(f"x_in{u}_") for u in range(G)]
        w1d_zero = sem("w1d_zero")
        w_in = sem("w_in")
        es_in = [sem(f"es_in{b}_") for b in range(2)]
        h_psum, h_ready, w_psum, w_ready = sem("h_psum"), sem("h_ready"), sem("w_psum"), sem("w_ready")
        w_out = [sem(f"w_out{b}_") for b in range(2)]
        ea_in = [sem(f"ea_in{b}_") for b in range(2)]
        eh_psum = sem("eh_psum")
        eh_ready = sem("eh_ready")
        ae_psum = sem("ae_psum")
        erow_ready = sem("erow_ready")
        erow_out = [sem(f"erow_out{b}_") for b in range(2)]
        wa_ready = sem("wa_ready")
        wa_own = sem("wa_own")
        block = ctx.enter_context(nc.Block())
        n_in = 16 * (32 if layer == 0 else 7)

        @block.sync
        def _(sp):
            if layer:
                sp.sem_inc(ln.free, 1)
            sp.wait_ge(w1d_zero, 2)
            for h in range(2):
                half = slice(64 * h, 64 * h + 64)
                sp.dma_start(w1d[half, half], a["L2_gnn_W_fc1"]).then_inc(w_in, 16)
                for n, column in enumerate((2, 0, 1, 3)):
                    sp.dma_start(w2d[half, P * h + 32 * n:P * h + 32 * n + 32],
                                 a["L2_gnn_W_fc2"][:, 32 * column:32 * column + 32]).then_inc(w_in, 16)
            wrows = t["w"].rearrange("(b n p) f -> b p n f", n=WB, p=P)
            e4rows = a["ea4"].rearrange("(b n p) f -> b p n f", n=WB, p=P)

            def load_es(i, b):
                n = layer * BODIES + i
                sp.dma_start(es[:, b], a["ea64T"][:, bass.ds(n * (2 * P), 2 * P)]).then_inc(es_in[b], 16)
                sp.dma_start(wrow[:, b, :, D:WW], e4rows[bass.ds(n, 1)].rearrange("o p n f -> (o p) n f")).then_inc(es_in[b], 16)

            def store_w(i, b):
                sp.wait_ge(w_ready, i + 2)
                sp.dma_start(wrows[bass.ds(layer * BODIES + i, 1)].rearrange("o p n f -> (o p) n f"),
                             wrow[:, b]).then_inc(w_out[b], 16)

            for b in range(2):
                load_es(b, b)
            sp.dma_start(wl[:], a[f"L0_gnn_Wl{layer}"].rearrange("(k p) n -> p k n", p=P)).then_inc(setup_in, 16)
            sp.dma_start(wr[:], a[f"L0_gnn_Wr{layer}"].rearrange("(k p) n -> p k n", p=P)).then_inc(setup_in, 16)
            for n, name in enumerate(("bl", "g", "b")):
                sp.dma_start(vecs[:, n], a[f"L0_gnn_{name}{layer}"].rearrange("(f p) -> p f", p=P),
                             allow_slow_non_contiguous=True).then_inc(setup_in, 16)
            if layer == 0:
                sp.dma_start(rcb[:], t["rc"].partition_broadcast(P)).then_inc(setup_in, 16)
                sp.dma_start(xT[:], a["xT"]).then_inc(setup_in, 16)
                for n in range(8):
                    part = slice(16 * n, 16 * n + 16)
                    sp.dma_start(wep1[part], a["L3_gnn_W_ep"]).then_inc(setup_in, 16)
                    sp.dma_start(bep[part], a["L3_gnn_b_ep"].rearrange("(p o) -> p o", o=1)).then_inc(setup_in, 16)
                    sp.dma_start(wedge[part], a["L3_gnn_W_edge"]).then_inc(setup_in, 16)
                sp.dma_start(atte[:], a["L3_gnn_att_edge"].rearrange("h c -> (h c)").partition_broadcast(P)).then_inc(setup_in, 16)
                flat = t["edge"].rearrange("r k -> (r k)").rearrange("(b p k) -> b p k", p=P, k=EF * EB // P)
                src = a["src"].rearrange("(b p g) -> b p g", p=P, g=EB // P)

                def load_block(i, b):
                    sp.dma_start(ea[:, b], a["ea16T"][:, bass.ds((2 * i + b) * P, P)]).then_inc(ea_in[b], 16)
                    sp.dma_start(esrc[:, b], src[bass.ds(2 * i + b, 1)].rearrange("o p g -> (o p) g")).then_inc(ea_in[b], 16)

                for b in range(2):
                    load_block(0, b)
                with sp.Fori(0, BODIES // 2) as i:
                    for b in range(2):
                        store_w(2 * i + b, b)
                        sp.wait_ge(erow_ready, 2 * i + b + 2)
                        sp.dma_start(flat[bass.ds(2 * i + b, 1)].rearrange("o p k -> (o p) k"),
                                     erow[:, b].rearrange("p g f -> p (g f)")).then_inc(erow_out[b], 16)
                        sp.wait_ge(erow_out[b], 16 * i + 16)
                        load_block(i + 1, b)
                        sp.wait_ge(w_out[b], 16 * i + 16)
                        load_es(2 * i + b + 2, b)
                for n in range(TILES):
                    sp.wait_ge(staged, n + 1)
                    sp.dma_start(t["ys"][n * P:(n + 1) * P, :],
                                 ystage[:, n % G].rearrange("p s d -> p (s d)")).then_inc(stored[n % G], 16)
                for u in range(G):
                    sp.wait_ge(stored[u], 16 * GROUPS)
                for b in range(2):
                    sp.wait_ge(erow_out[b], 16 * (BODIES // 2))
                    sp.wait_ge(ea_in[b], 32 * (BODIES // 2 + 1))
            else:
                sp.dma_start(wp[:], a["L0_gnn_Wp"].rearrange("(k p) n -> p k n", p=P)).then_inc(setup_in, 16)
                sp.dma_start(bp[:], a["L0_gnn_bp"].rearrange("(o n) -> o n", o=1)).then_inc(setup_in, 16)
                with sp.Fori(0, BODIES // 2) as i:
                    for b in range(2):
                        store_w(2 * i + b, b)
                        sp.wait_ge(w_out[b], 16 * i + 16)
                        load_es(2 * i + b + 2, b)
                for n in range(TILES):
                    if n >= G:
                        sp.wait_ge(staged, n - G + 1)
                    sp.dma_start(xin[:, n % G], a["x"][n * P:(n + 1) * P, :]).then_inc(x_in[n % G], 16)
                rows_out = t["x1"].rearrange("(g u p) f -> g p u f", p=P, u=G)
                with sp.Fori(0, GROUPS) as g:
                    sp.wait_ge(ln.ready, g + 1)
                    sp.dma_start(rows_out[bass.ds(g, 1)].rearrange("o p u f -> (o p) u f"), x1[:]).then_inc(stored[0], 16)
                    sp.wait_ge(stored[0], 16 * g + 16)
                    sp.sem_inc(ln.free, 1)
            for b in range(2):
                sp.wait_ge(es_in[b], 32 * (BODIES // 2 + 1))
                sp.wait_ge(w_out[b], 16 * (BODIES // 2))

        @block.gpsimd
        def _(pool):
            table = t["xs"] if layer == 0 else t["ys"]
            with pool.Fori(0, BODIES // 2) as i:
                for h in range(2):
                    pool.wait_ge(idx_ready, 2 * i + h + 1)
                    for u in range(U):
                        pool.wait_ge(step_done, U * (2 * i + h) + u + 1)
                        pool.sem_inc(pool_go, 1)
                        pool.indirect_dma_start(rows[:, u, :], None, table,
                                                bass.IndirectOffsetOnAxis(ap=idx[:, h, u:u + 1], axis=0)).then_inc(gathered[u], 16)

        @block.scalar
        def _(act):
            act.wait_ge(setup_in, n_in)
            with act.Fori(0, BODIES // 2) as i:
                for h in range(2):
                    n = U * (2 * i + h)
                    act.wait_ge(step_done, n + 1)
                    act.copy(idx[:, h], s["srcS"][:, bass.ds(n, U)]).then_inc(idx_ready, 1)
                    act.wait_ge(h_psum, 2 * i + h + 1)
                    act.activation(hT[:], ps[:, 5, 0:2 * P], ACT.Silu, scale=1.0 / 8).then_inc(h_ready, 1)
                    act.wait_ge(w_psum, 2 * i + h + 1)
                    act.activation(wrow[:, h, :, 0:D], ps[:, 7, :].rearrange("p (n d) -> p n d", n=WB), ACT.Copy,
                                   scale=SILU_NORM / 8).then_inc(w_ready, 1)
            for c in range(NCH):
                for f in range(2):
                    act.wait_ge(dense_ready, 2 * c + (2 if layer else f + 1))
                    n = 2 * c + f
                    dst = yT if layer == 0 else agg
                    act.activation(dst[:, f, c * CH:(c + 1) * CH], ps[:, n % 4, 0:CH], ACT.Relu,
                                   bias=vecs[:, 0, f:f + 1]).then_inc(dense_free, 1)
            act.wait_ge(var_ready, 1)
            act.activation(scale[:], scale[:], ACT.Sqrt).then_inc(std_ready, 1)
            if layer:
                ln.scalar(act)
            else:
                for n in range(TILES):
                    act.wait_ge(turned, n + 1)
                    if n >= G:
                        act.wait_ge(stored[n % G], 16 * (n // G))
                    act.copy(ystage[:, n % G, 0], ps[:, n % G, 0:HID]).then_inc(hi_ready, 1)
                    act.wait_ge(rest_ready, n + 1)
                    act.copy(ystage[:, n % G, 1], yrest[:, n % 2]).then_inc(mid_ready, 1)

        @block.tensor
        def _(pe):
            pe.sem_inc(step_done, U)
            pe.wait_ge(setup_in, n_in)
            if layer == 0:
                pe.wait_ge(wa_ready, 1)

            def steps(i, lo, hi, h):
                for u in range(lo, hi):
                    n = 2 * U * i + U * h + u + 1
                    pe.wait_ge(gathered[u], 16 * (2 * i + h) + 16)
                    pe.wait_ge(onehot_ready, n)
                    pe.wait_ge(added, n)
                    for k in range(KB):
                        for part in range(3):
                            at = part * W + k * P
                            last = pe.matmul(ps[:, u % 4, k * P:(k + 1) * P], rows[:, u, at:at + P], onehot[:, u],
                                             start=(part == 0), stop=(part == 2))
                    last.then_inc(step_done, 1)

            pe.wait_ge(w_in, 160)
            with pe.Fori(0, BODIES // 2) as i:
                for h in range(2):
                    pe.wait_ge(es_in[h], 32 * i + 32)
                    pe.wait_ge(h_ready, 2 * i + h + 1)
                    pe.matmul(ps[:, 5, 0:2 * P], w1d[:], es[:, h], start=True, stop=True).then_inc(h_psum, 1)
                    steps(i, 0, 4, h)
                    pe.wait_ge(h_ready, 2 * i + h + 2)
                    pe.wait_ge(w_ready, 2 * i + h + 1)
                    for n in range(2):
                        last = pe.matmul(ps[:, 7, 2 * n * P:(2 * n + 2) * P], hT[:, n * P:(n + 1) * P], w2d[:],
                                         start=True, stop=True)
                    last.then_inc(w_psum, 1)
                    if layer == 0:
                        pe.wait_ge(ea_in[h], 32 * i + 32)
                        pe.wait_ge(eh_ready, 2 * i + h + 1)
                        pe.matmul(ps[:, 4, 0:P], wep[:].rearrange("p n f -> p (n f)"), ea[:, h], start=True,
                                  stop=True).then_inc(eh_psum, 1)
                    steps(i, 4, 8, h)
                    if layer == 0:
                        pe.wait_ge(eh_ready, 2 * i + h + 2)
                        pe.wait_ge(erow_ready, 2 * i + h + 1)
                        pe.matmul(ps[:, 6, 0:32], eh[:], wa[:].rearrange("p n f -> p (n f)"), start=True,
                                  stop=True).then_inc(ae_psum, 1)
            pe.wait_ge(agg_ready, 1)
            for c in range(NCH):
                for f in range(2):
                    n = 2 * c + f
                    if n >= 4:
                        pe.wait_ge(dense_free, n - 3)
                    cols = slice(c * CH, (c + 1) * CH)
                    for k in range(KB):
                        pe.matmul(ps[:, n % 4, 0:CH], wl[:, k, f * P:(f + 1) * P], agg[:, k, cols], start=(k == 0), stop=False)
                    for k in range(KB):
                        last = pe.matmul(ps[:, n % 4, 0:CH], wr[:, k, f * P:(f + 1) * P], own[:, k, cols],
                                         start=False, stop=(k == KB - 1))
                    last.then_inc(dense_ready, 1)
            pe.wait_ge(y_ready, 1)
            for n in range(TILES):
                if n >= G:
                    pe.wait_ge(staged, n - G + 1)
                cols = slice(n * P, (n + 1) * P)
                if layer == 0:
                    for f in range(2):
                        last = pe.transpose(ps[:, n % G, f * P:(f + 1) * P], yT[:, f, cols], s["ident"][:])
                else:
                    for f in range(2):
                        pe.matmul(ps[:, n % G, 0:D], agg[:, f, cols], wp[:, f], start=(f == 0), stop=False)
                    last = pe.matmul(ps[:, n % G, 0:D], s["ones"][0:1, :], bp[:], start=False, stop=True)
                last.then_inc(turned, 1)

        @block.vector
        def _(dve):
            dve.memset(w1d[:], 0.0).then_inc(w1d_zero, 1)
            dve.memset(w2d[:], 0.0).then_inc(w1d_zero, 1)
            dve.sem_inc(h_ready, 1)
            dve.sem_inc(w_ready, 1)
            dve.wait_ge(setup_in, n_in)
            if layer == 0:
                do = Chain(dve, wa_own)
                do(dve.tensor_tensor(wedge[:], wedge[:], atte[:], ALU.mult))
                do(dve.tensor_reduce(wa1[:], wedge[:].rearrange("p (h c) -> p h c", h=4), AX_X, ALU.add))
                do(dve.tensor_tensor(wep[:], broadcast(wep1[:], [P, 8, 16], 1), broadcast(s["eighth"][:], [P, 8, 16], 2), ALU.mult))
                dve.tensor_tensor(wa[:], broadcast(wa1[:], [P, 8, 4], 1), broadcast(s["eighth"][:], [P, 8, 4], 2),
                                  ALU.mult).then_inc(wa_ready, 1)
                dve.sem_inc(eh_ready, 1)
                dve.sem_inc(erow_ready, 1)
            dve.memset(agg[:], 0.0).then_inc(agg_zero, 1)
            dve.wait_ge(agg_zero, 1)
            dve.sem_inc(added, 4)
            def add(i, h, u, tile):
                dve.wait_ge(step_done, 2 * U * i + U * h + u + 1 + U)
                dve.wait_ge(added, 2 * U * i + U * h + u + 4)
                into = agg[:, :, bass.ds(tile * P, P)]
                dve.tensor_tensor(into, into, ps[:, u % 4, 0:W].rearrange("p (k n) -> p k n", n=P),
                                  ALU.add).then_inc(added, 1)

            with dve.Fori(0, BODIES // 2) as i:
                for h in range(2):
                    tiles = []
                    for u in range(U):
                        n = 2 * U * i + U * h + u
                        if u % 4 == 0:
                            tiles += node_tiles(dve, s, 4 * i + 2 * h + u // 4)
                        dve.wait_ge(step_done, n + 1)
                        dve.tensor_scalar(onehot[:, u], s["iota"][:], s["dstS"][:, bass.ds(n, 1)], None,
                                          ALU.is_equal).then_inc(onehot_ready, 1)
                        if u >= 2:
                            add(i, h, u - 2, tiles[u - 2])
                        if layer == 0 and u == 6:
                            dve.wait_ge(eh_psum, 2 * i + h + 1)
                            dve.tensor_scalar(eh[:], ps[:, 4, 0:P], bep[:, 0:1], 0.0,
                                              ALU.add, ALU.max).then_inc(eh_ready, 1)
                    for u in (U - 2, U - 1):
                        add(i, h, u, tiles[u])
                    if layer == 0:
                        dve.wait_ge(ea_in[h], 32 * i + 32)
                        dve.wait_ge(ae_psum, 2 * i + h + 1)
                        dve.tensor_copy(erow[:, h, :, 1:EF], ps[:, 6, 0:32].rearrange("p (g f) -> p g f", f=4))
                        dve.tensor_copy(erow[:, h, :, 0], esrc[:, h]).then_inc(erow_ready, 1)
            do = Chain(dve, stats_own)
            dve.wait_ge(added, STEPS + 4)
            for k in range(KB):
                do.put(dve.tensor_tensor(agg[:, k], agg[:, k], rcb[:], ALU.mult))
            do.sync()
            dve.sem_inc(agg_ready, 1)
            h_ = yT if layer == 0 else agg
            for c in range(NCH):
                for f in range(2):
                    dve.wait_ge(dense_free, 2 * c + f + 1)
                    do.put(dve.bn_stats(stats[:, f, c], h_[:, f, c * CH:min((c + 1) * CH, N)]))
            do.sync()
            for f in range(2):
                do.put(dve.bn_aggr(mv[:, f], stats[:, f].rearrange("p c s -> p (c s)")))
            do.sync()
            do(dve.tensor_scalar(scale[:], mv[:, :, 1], 1e-5, None, ALU.add))
            dve.sem_inc(var_ready, 1)
            dve.wait_ge(std_ready, 1)
            do(dve.reciprocal(scale[:], scale[:]))
            do(dve.tensor_tensor(scale[:], scale[:], vecs[:, 1], ALU.mult))
            do(dve.tensor_tensor(shift[:], mv[:, :, 0], scale[:], ALU.mult))
            do(dve.tensor_tensor(shift[:], vecs[:, 2], shift[:], ALU.subtract))
            for f in range(2):
                do.put(dve.tensor_scalar(h_[:, f], h_[:, f], scale[:, f:f + 1], shift[:, f:f + 1], ALU.mult, ALU.add))
            do.sync()
            dve.sem_inc(y_ready, 1)
            for n in range(TILES):
                dve.wait_ge(turned, n + 1)
                if layer == 0:
                    dve.wait_ge(hi_ready, n + 1)
                    dve.tensor_tensor(yrest[:, n % 2], ps[:, n % G, 0:HID], ystage[:, n % G, 0], ALU.subtract).then_inc(rest_ready, 1)
                    dve.wait_ge(mid_ready, n + 1)
                    dve.tensor_tensor(ystage[:, n % G, 2], yrest[:, n % 2], ystage[:, n % G, 1], ALU.subtract).then_inc(staged, 1)
                else:
                    dve.wait_ge(x_in[n % G], 16 * (n // G + 1))
                    dve.scalar_tensor_tensor(v[:, n], ps[:, n % G, 0:D], 0.0, xin[:, n % G], ALU.max, ALU.add).then_inc(staged, 1)
            if layer:
                dve.memset(x1[:], 0.0).then_inc(staged, 1)
                dve.wait_ge(staged, TILES + 1)
                ln.vector(dve, v, lambda g, u: x1[:, u], sumsq=True)


class Rounds:

    SHIFT_OPS = 6

    def __init__(self, ctx, nc, sem, s, name, edge_table, table, width, fields):
        sb = lambda n, shape, dt=F32: ctx.enter_context(nc.sbuf_tensor(f"{name}_{n}", shape, dt))
        self.name, self.s, self.edge_table, self.table, self.fields = name, s, edge_table, table, fields
        self.at_row = sb("at_row", [P, 2, G])
        self.row_idx = sb("row_idx", [P, 2, G], I32)
        self.raw = sb("raw", [P, G, 2, RUN * EF])
        self.edges = sb("edges", [P, G, 2 * RUN, fields])
        self.bits = sb("bits", [P, 5, G], I32)
        self.idx = sb("idx", [P, R, G], I32)
        self.rows = sb("rows", [P, R, G, width])
        self.pool_group, self.pool_chunk, self.pool_round = sem("pool_group"), sem("pool_chunk"), sem("pool_round")
        self.raw_in = [sem(f"raw_in{n}") for n in range(2)]
        self.raw_free, self.edges_ready, self.shift_own = sem("raw_free"), sem("edges_ready"), sem("shift_own")
        self.round_done, self.took = sem("round_done"), sem("took")
        self.gathered = [sem(f"gathered{r}") for r in range(R)]

    def group(self, eng, g):
        return [eng.value_load(self.s["rounds"][0:1, n, bass.ds(g, 1)], min_val=0, max_val=MAXB) for n in range(4)]

    def bodies(self, eng, limit, c, q):
        eng.reg_alu(limit, c * CBODY + CBODY, q, ALU.min)
        return c * CBODY, eng.snap(limit).with_bounds(min_val=0, max_val=MAXB)

    def gather(self, pool):
        limit = pool.alloc_register(f"{self.name}_chunk_end")
        with pool.Fori(0, GROUPS) as g:
            q, q_before, chunks, c_before = self.group(pool, g)
            do = Chain(pool, self.pool_group, g * 2, self.took)
            do(pool.tensor_copy(self.at_row[:, 0], self.s["srow"][:, bass.ds(g * G, G)]))
            do(pool.tensor_scalar(self.at_row[:, 1], self.at_row[:, 0], 1.0, None, ALU.add))
            with pool.Fori(0, chunks) as c:
                ci = c_before + c
                do = Chain(pool, self.pool_chunk, ci * 3, self.took)
                do(pool.tensor_scalar(self.at_row[:], self.at_row[:], float(RUNS - 1), None, ALU.min))
                pool.wait_ge(self.raw_free, ci + 1)
                pool.sem_inc(self.took, 1)
                do(pool.tensor_copy(self.row_idx[:], self.at_row[:]))
                do(pool.tensor_scalar(self.at_row[:], self.at_row[:], 1.0, None, ALU.add))
                for n in range(2):
                    for u in range(G):
                        pool.indirect_dma_start(
                            self.raw[:, u, n, :], None, self.edge_table,
                            bass.IndirectOffsetOnAxis(ap=self.row_idx[:, n, u:u + 1], axis=0)).then_inc(self.raw_in[n], 16)
                pool.wait_ge(self.edges_ready, ci + 1)
                pool.sem_inc(self.took, 1)
                lo, hi = self.bodies(pool, limit, c, q)
                with pool.Fori(lo, hi) as j:
                    place = pool.snap((j - lo) * R).with_bounds(min_val=0, max_val=RUN - R)
                    for r in range(R):
                        n = (q_before + j) * R + r + 1
                        pool.wait_ge(self.round_done, n)
                        pool.sem_inc(self.took, 1)
                        pool.tensor_copy(self.idx[:, r, :],
                                         self.edges[:, :, bass.ds(place + r, 1), 0].rearrange("p u o -> p (u o)")
                                         ).then_inc(self.pool_round, 1)
                        pool.wait_ge(self.pool_round, n)
                        pool.sem_inc(self.took, 1)
                        for u in range(G):
                            pool.indirect_dma_start(
                                self.rows[:, r, u, :], None, self.table,
                                bass.IndirectOffsetOnAxis(ap=self.idx[:, r, u:u + 1], axis=0)).then_inc(self.gathered[r], 16)

    def shift(self, dve, ci):
        do = Chain(dve, self.shift_own, ci * self.SHIFT_OPS, self.took)
        raw = self.raw[:].rearrange("p u n (k f) -> p u (n k) f", f=EF)[:, :, :, 0:self.fields]
        for n in range(2):
            dve.wait_ge(self.raw_in[n], (ci + 1) * (16 * G))
        do(dve.tensor_copy(self.edges[:], raw))
        dve.sem_inc(self.raw_free, 1)
        width = 2 * RUN
        for b in (4, 3, 2, 1, 0):
            width -= 1 << b
            mask = self.bits[:, b].unsqueeze(2).unsqueeze(3).broadcast_to([P, G, width, self.fields])
            do(dve.copy_predicated(self.edges[:, :, 0:width], mask, self.edges[:, :, (1 << b):(1 << b) + width]))
        dve.sem_inc(self.edges_ready, 1)


def moebius(nc, a, t, s):
    EPS = 1e-7
    with ExitStack() as ctx:
        def sb(name, shape, dt=F32):
            return ctx.enter_context(nc.sbuf_tensor(f"mb_{name}", shape, dt))

        sem = Semaphores(nc, ctx, "mb_")
        xd = sb("xd", [P, TILES, XW])
        fold = sb("fold", [P, TILES, D])
        cz_all = sb("cz_all", [P, TILES])
        rd = Rounds(ctx, nc, sem, s, "mb", t["edge"], t["x1"], XW, 1)
        ln = LayerNorm(ctx, nc, sem, "mb")
        xg = sb("xg", [P, G, XW])
        u_ = sb("u", [P, G, D])
        cz = sb("cz", [P, 2, G])
        cz1 = sb("cz1", [P, 2, G])
        cz2 = sb("cz2", [P, 2, G])
        n2 = sb("n2", [P, G])
        y2 = sb("y2", [P, G])
        dg = sb("dg", [P, G])
        kk = sb("kk", [P, 2])
        junk = sb("junk", [P, 2 * G, D])
        dots = sb("dots", [P, 2, G])
        q_ = sb("q", [P, G])
        w = [sb(f"w{n}", [P, 2, G]) for n in range(9)]
        v = [sb(f"v{n}", [P, G]) for n in range(10)]
        bm = sb("bm", [P, 2, 2, G])
        gm = sb("gm", [P, G])
        scaled = sb("scaled", [P, G, D])
        xout = sb("xout", [P, G, D])
        pidx = sb("pidx", [P, G], I32)

        nodes_in = sem("nodes_in")
        grp, chk, bod = sem("group_own"), sem("chunk_own"), sem("body_own")
        gm_ready, scaled_ready = sem("gm_ready"), sem("scaled_ready")
        fin = sem("final_own")
        f_ready, f_back = sem("f_ready"), sem("f_back")
        pidx_own, scattered = sem("pidx_own"), sem("scattered")
        block = ctx.enter_context(nc.Block())

        @block.gpsimd
        def _(pool):
            pool.sem_inc(ln.free, 1)
            for n in range(TILES):
                pool.indirect_dma_start(xd[:, n, :], None, t["x1"],
                                        bass.IndirectOffsetOnAxis(ap=s["perm"][:, n:n + 1], axis=0)).then_inc(nodes_in, 16)
            rd.gather(pool)
            with pool.Fori(0, GROUPS) as g:
                pool.tensor_copy(pidx[:], s["perm"][:, bass.ds(g * G, G)]).then_inc(pidx_own, 1)
                pool.wait_ge(pidx_own, g + 1)
                pool.wait_ge(ln.ready, g + 1)
                pool.sem_inc(rd.took, 1)
                for u in range(G):
                    pool.indirect_dma_start(t["x2"][:, :], bass.IndirectOffsetOnAxis(ap=pidx[:, u:u + 1], axis=0),
                                            xout[:, u, :], None).then_inc(scattered, 16)
                pool.wait_ge(scattered, (g + 1) * (16 * G))
                pool.sem_inc(ln.free, 1)

        @block.scalar
        def _(act):
            with act.Fori(0, GROUPS) as g:
                q, q_before, chunks, c_before = rd.group(act, g)
                with act.Fori(0, q) as j:
                    for r in range(R):
                        act.wait_ge(gm_ready, (q_before + j) * R + r + 1)
                        for u in range(G):
                            last = act.activation(scaled[:, u], rd.rows[:, r, u, 0:D], ACT.Copy, scale=gm[:, u:u + 1])
                        last.then_inc(scaled_ready, 1)
            with act.Fori(0, GROUPS) as g:
                act.wait_ge(f_ready, g * 3 + 1)
                act.activation(v[1][:], v[0][:], ACT.Sqrt).then_inc(f_back, 1)
                act.wait_ge(f_ready, g * 3 + 2)
                act.activation(v[1][:], v[0][:], ACT.Ln).then_inc(f_back, 1)
                act.wait_ge(f_ready, g * 3 + 3)
                act.activation(v[1][:], v[0][:], ACT.Tanh, scale=0.5).then_inc(f_back, 1)
            ln.scalar(act)

        @block.vector
        def _(dve):
            limit = dve.alloc_register("mb_chunk_end")
            dve.wait_ge(nodes_in, 16 * TILES)
            dve.sem_inc(rd.raw_free, 1)
            dve.sem_inc(rd.round_done, R)
            GROUP_OPS, HALF_OPS, ROUND_OPS = 11, 32, 34
            BODY_OPS = 2 * HALF_OPS + R * ROUND_OPS
            pair = [P, 2, G]
            with dve.Fori(0, GROUPS) as g:
                q, q_before, chunks, c_before = rd.group(dve, g)
                do = Chain(dve, grp, g * GROUP_OPS, rd.took)
                mine = bass.ds(g * G, G)
                do.put(dve.tensor_copy(xg[:], xd[:, mine, :]))
                do.put(dve.tensor_copy(y2[:], xd[:, mine, D]))
                do.put(dve.tensor_copy(dg[:], s["sdeg"][:, mine]))
                do.put(dve.tensor_copy(rd.bits[:], s["sbit"][:, :, mine]))
                do.put(dve.memset(u_[:], 0.0))
                do.put(dve.memset(cz[:], 0.0))
                do.put(dve.memset(n2[:], 0.0))
                do.put(dve.memset(kk[:, 0:1], 0.0))
                do(dve.memset(kk[:, 1:2], 1.0))
                with dve.Fori(0, chunks) as c:
                    rd.shift(dve, c_before + c)
                    lo, hi = rd.bodies(dve, limit, c, q)
                    with dve.Fori(lo, hi) as j:
                        do_b = Chain(dve, bod, (q_before + j) * BODY_OPS)
                        y2b = y2[:].unsqueeze(1).broadcast_to(pair)
                        for half in range(2):
                            start = do_b.n
                            rows = rd.rows[:, 2 * half:2 * half + 2]
                            for r in range(2):
                                dve.wait_ge(rd.gathered[2 * half + r], (q_before + j + 1) * (16 * G))
                                for u in range(G):
                                    do_b.put(dve.tensor_tensor_reduce(
                                        out=junk[:, r * G + u], in0=rows[:, r, u, 0:D], in1=xg[:, u, 0:D], scale=1.0, scalar=0.0,
                                        op0=ALU.mult, op1=ALU.add, accum_out=dots[:, r, u:u + 1]))
                            t0, an, pr, den, rm, valid, al, nn, m2 = w
                            xs2 = rows[:, :, :, D]
                            do_b.put(dve.tensor_tensor(valid[:], dg[:].unsqueeze(1).broadcast_to(pair),
                                                       kk[:].unsqueeze(2).broadcast_to(pair), ALU.is_gt))
                            do_b(dve.tensor_tensor(pr[:], xs2, y2b, ALU.mult))
                            do_b.put(dve.tensor_scalar(kk[:], kk[:], 2.0, None, ALU.add))
                            do_b(dve.tensor_scalar(t0[:], dots[:], -2.0, 1.0, ALU.mult, ALU.add))
                            do_b.put(dve.tensor_tensor(an[:], t0[:], y2b, ALU.add))
                            do_b(dve.tensor_tensor(den[:], pr[:], t0[:], ALU.add))
                            do_b.put(dve.scalar_tensor_tensor(nn[:], an[:], -1.0, xs2, ALU.add, ALU.add))
                            do_b(dve.tensor_scalar(rm[:], den[:], EPS, None, ALU.max))
                            do_b(dve.reciprocal(rm[:], rm[:]))
                            do_b(dve.tensor_tensor(rm[:], rm[:], valid[:], ALU.mult))
                            do_b.put(dve.tensor_tensor(al[:], an[:], rm[:], ALU.mult))
                            do_b.put(dve.scalar_tensor_tensor(bm[:, :, 0], xs2, -1.0, rm[:], ALU.add, ALU.mult))
                            do_b(dve.tensor_tensor(m2[:], nn[:], den[:], ALU.mult))
                            do_b.put(dve.tensor_tensor(t0[:], al[:], dots[:], ALU.mult))
                            do_b.put(dve.tensor_tensor(an[:], bm[:, :, 0], y2b, ALU.mult))
                            do_b(dve.tensor_tensor(m2[:], m2[:], rm[:], ALU.mult))
                            do_b.put(dve.tensor_tensor(m2[:], m2[:], rm[:], ALU.mult))
                            do_b(dve.tensor_tensor(bm[:, :, 1], t0[:], an[:], ALU.add))
                            HALF = do_b.n - start
                            assert HALF <= HALF_OPS, HALF
                            for r in range(2):
                                start = do_b.n
                                n = (q_before + j) * R + 2 * half + r + 1
                                alr, m2r = al[:, r], m2[:, r]
                                for u in range(G):
                                    do_b.put(dve.tensor_tensor_reduce(
                                        out=junk[:, r * G + u], in0=rows[:, r, u, 0:D], in1=u_[:, u], scale=1.0, scalar=0.0,
                                        op0=ALU.mult, op1=ALU.add, accum_out=q_[:, u:u + 1]))
                                h1, h2, xy, aa, ww, dd, rr, ap, nb, n2b = v
                                do_b.put(dve.tensor_tensor(h1[:], cz[:, 0], dots[:, r], ALU.mult))
                                do_b.put(dve.tensor_tensor(h2[:], cz[:, 1], bm[:, r, 0], ALU.mult))
                                do_b(dve.tensor_tensor(ww[:], n2[:], m2r, ALU.mult))
                                do_b(dve.tensor_tensor(h1[:], h1[:], q_[:], ALU.add))
                                do_b(dve.tensor_tensor(h1[:], h1[:], alr, ALU.mult))
                                do_b(dve.tensor_tensor(xy[:], h1[:], h2[:], ALU.add))
                                do_b(dve.tensor_scalar(xy[:], xy[:], 2.0, 1.0, ALU.mult, ALU.add))
                                do_b.put(dve.tensor_tensor(aa[:], xy[:], m2r, ALU.add))
                                do_b(dve.tensor_tensor(dd[:], xy[:], ww[:], ALU.add))
                                do_b(dve.tensor_scalar(rr[:], dd[:], EPS, None, ALU.max))
                                do_b(dve.reciprocal(rr[:], rr[:]))
                                do_b.put(dve.scalar_tensor_tensor(nb[:], n2[:], -1.0, rr[:], ALU.add, ALU.mult))
                                do_b(dve.tensor_tensor(ap[:], aa[:], rr[:], ALU.mult))
                                dve.scalar_tensor_tensor(gm[:], alr, -1.0, nb[:], ALU.mult, ALU.mult).then_inc(gm_ready, 1)
                                do_b.put(dve.scalar_tensor_tensor(n2b[:], aa[:], -1.0, n2[:], ALU.add, ALU.add))
                                do_b.put(dve.tensor_tensor(cz1[:], cz[:], ap[:].unsqueeze(1).broadcast_to(pair), ALU.mult))
                                do_b(dve.scalar_tensor_tensor(cz2[:], bm[:, r], -1.0, nb[:].unsqueeze(1).broadcast_to(pair),
                                                              ALU.mult, ALU.mult))
                                do_b.put(dve.tensor_tensor(n2b[:], n2b[:], dd[:], ALU.mult))
                                do_b(dve.tensor_tensor(cz[:], cz1[:], cz2[:], ALU.add))
                                do_b(dve.tensor_tensor(n2b[:], n2b[:], rr[:], ALU.mult))
                                do_b(dve.tensor_tensor(n2[:], n2b[:], rr[:], ALU.mult))
                                dve.wait_ge(scaled_ready, n)
                                for u in range(G):
                                    do_b.put(dve.scalar_tensor_tensor(u_[:, u], u_[:, u], ap[:, u:u + 1], scaled[:, u], ALU.mult, ALU.add))
                                do_b.sync()
                                dve.sem_inc(rd.round_done, 1)
                                ROUND = do_b.n - start
                        assert do_b.n == BODY_OPS, (HALF, ROUND)
                do.put(dve.tensor_copy(fold[:, mine], u_[:]))
                do(dve.tensor_copy(cz_all[:, mine], cz[:, 0]))
                assert do.n == GROUP_OPS, do.n
            FINAL_OPS = 67
            with dve.Fori(0, GROUPS) as g:
                do = Chain(dve, fin, g * FINAL_OPS, rd.took)
                mine = bass.ds(g * G, G)
                arg, back, nrm, nc_, rn, ff, aa, dd, xy, yy = v
                do.put(dve.tensor_copy(xg[:], xd[:, mine, :]))
                do.put(dve.tensor_copy(y2[:], xd[:, mine, D]))
                do.put(dve.tensor_scalar(dg[:], s["sdeg"][:, mine], 1.0, None, ALU.max))
                do.put(dve.tensor_copy(u_[:], fold[:, mine]))
                do(dve.tensor_copy(cz[:, 0], cz_all[:, mine]))
                for u in range(G):
                    do.put(dve.scalar_tensor_tensor(u_[:, u], xg[:, u, 0:D], cz[:, 0, u:u + 1], u_[:, u], ALU.mult, ALU.add))
                do.put(dve.reciprocal(dg[:], dg[:]))
                do.sync()
                for u in range(G):
                    do.put(dve.tensor_tensor_reduce(out=junk[:, u], in0=u_[:, u], in1=u_[:, u], scale=1.0, scalar=0.0,
                                                    op0=ALU.mult, op1=ALU.add, accum_out=arg[:, u:u + 1]))
                    do.put(dve.tensor_tensor_reduce(out=junk[:, G + u], in0=u_[:, u], in1=xg[:, u, 0:D], scale=1.0, scalar=0.0,
                                                    op0=ALU.mult, op1=ALU.add, accum_out=xy[:, u:u + 1]))
                do.sync()
                do(dve.tensor_copy(n2[:], arg[:]))
                dve.sem_inc(f_ready, 1)
                dve.wait_ge(f_back, g * 3 + 1)
                do(dve.tensor_copy(nrm[:], back[:]))
                do(dve.tensor_scalar(nc_[:], nrm[:], EPS, float(np.float32(1.0 - EPS)), ALU.max, ALU.min))
                do.put(dve.tensor_scalar(aa[:], nc_[:], -1.0, 1.0, ALU.mult, ALU.add))
                do(dve.tensor_scalar(dd[:], nc_[:], 1.0, None, ALU.add))
                do.put(dve.reciprocal(rn[:], nc_[:]))
                do(dve.reciprocal(aa[:], aa[:]))
                do(dve.tensor_tensor(arg[:], dd[:], aa[:], ALU.mult))
                dve.sem_inc(f_ready, 1)
                dve.wait_ge(f_back, g * 3 + 2)
                do(dve.tensor_tensor(arg[:], back[:], dg[:], ALU.mult))
                dve.sem_inc(f_ready, 1)
                dve.wait_ge(f_back, g * 3 + 3)
                do(dve.tensor_tensor(ff[:], back[:], rn[:], ALU.mult))
                do(dve.tensor_scalar(nrm[:], nrm[:], EPS, None, ALU.is_gt))
                do(dve.tensor_tensor(ff[:], ff[:], nrm[:], ALU.mult))
                do.put(dve.tensor_tensor(xy[:], xy[:], ff[:], ALU.mult))
                do(dve.tensor_tensor(yy[:], n2[:], ff[:], ALU.mult))
                do.put(dve.tensor_scalar(xy[:], xy[:], 2.0, 1.0, ALU.mult, ALU.add))
                do(dve.tensor_tensor(yy[:], yy[:], ff[:], ALU.mult))
                do.put(dve.tensor_tensor(aa[:], xy[:], yy[:], ALU.add))
                do(dve.tensor_tensor(dd[:], y2[:], yy[:], ALU.mult))
                do(dve.tensor_tensor(dd[:], dd[:], xy[:], ALU.add))
                do(dve.tensor_scalar(dd[:], dd[:], EPS, None, ALU.max))
                do(dve.reciprocal(dd[:], dd[:]))
                do.put(dve.tensor_tensor(aa[:], aa[:], dd[:], ALU.mult))
                do(dve.scalar_tensor_tensor(nrm[:], y2[:], -1.0, dd[:], ALU.add, ALU.mult))
                do.put(dve.tensor_scalar(aa[:], aa[:], 1.0, None, ALU.add))
                do(dve.scalar_tensor_tensor(nrm[:], nrm[:], -1.0, ff[:], ALU.mult, ALU.mult))
                for u in range(G):
                    do.put(dve.tensor_scalar(scaled[:, u], u_[:, u], nrm[:, u:u + 1], None, ALU.mult))
                do.sync()
                for u in range(G):
                    do.put(dve.scalar_tensor_tensor(xout[:, u], xg[:, u, 0:D], aa[:, u:u + 1], scaled[:, u], ALU.mult, ALU.add))
                do.sync()
                do(dve.tensor_copy(fold[:, mine], xout[:]))
                assert do.n == FINAL_OPS, do.n
            ln.vector(dve, fold, lambda g, u: xout[:, u])


def equivariant(nc, a, t, s):
    MC = 320
    with ExitStack() as ctx:
        def sb(name, shape, dt=F32):
            return ctx.enter_context(nc.sbuf_tensor(f"eq_{name}", shape, dt))

        sem = Semaphores(nc, ctx, "eq_")
        ps = ctx.enter_context(nc.psum_tensor("eq_ps", [P, 8, 512], F32))
        x2 = sb("x2", [P, TILES, D])
        sc = sb("sc", [P, TILES, D])
        acc = sb("acc", [P, TILES, MC])
        cc = acc
        xt = sb("xt", [P, 2, P])
        m1 = sb("m1", [P, 2 * P])
        fst = sb("fst", [P, 4, D])
        attr = sb("attr", [P, TILES])
        fscale = sb("fscale", [P, TILES])
        idx = sb("idx", [P, 2, U], I32)
        frow = sb("frow", [P, U, D])
        wrow = sb("wrow", [P, U, WW])
        pb = sb("pb", [P, 4, 4, 2, 32])
        msg = sb("msg", [P, 4, MC])
        onehot = sb("onehot", [P, U, P])
        m2 = sb("m2", [P, 3, D + 1])
        rowscale = sb("rowscale", [P, 1])
        mt = sb("mt", [P, 2, 3, P])
        ang = sb("ang", [P, TILES])
        r_ = [sb(f"r{n}", [P, TILES]) for n in range(4)]
        ln = LayerNorm(ctx, nc, sem, "eq")
        xout = sb("xout", [P, G, D])

        x_in, w_zero, w_in = sem("x_in"), sem("w_zero"), sem("w_in")
        own = sem("own")
        xt_psum, xt_ready, f_psum, f_ready = sem("xt_psum"), sem("xt_ready"), sem("f_psum"), sem("f_ready")
        f_out = [sem(f"f_out{n}") for n in range(4)]
        f_all = sem("f_all")
        idx_ready, took, step_done, onehot_ready = sem("idx_ready"), sem("took"), sem("step_done"), sem("onehot_ready")
        gathered = [sem(f"gathered{u}") for u in range(U)]
        w_row_in = [sem(f"w_row_in{u}") for u in range(U)]
        pb_ready, msg_ready, added = sem("pb_ready"), sem("msg_ready"), sem("added")
        mt_psum, mt_ready, c_psum, c_ready = sem("mt_psum"), sem("mt_ready"), sem("c_psum"), sem("c_ready")
        trig, trig_back = sem("trig"), sem("trig_back")
        stored = sem("stored")
        block = ctx.enter_context(nc.Block())

        @block.sync
        def _(sp):
            sp.sem_inc(ln.free, 1)
            sp.dma_start(x2[:], t["x2"].rearrange("(t p) d -> p t d", p=P)).then_inc(x_in, 16)
            sp.dma_start(attr[:].unsqueeze(2), a["attr"].rearrange("(t p) o -> p t o", p=P),
                         allow_slow_non_contiguous=True).then_inc(x_in, 16)
            sp.wait_ge(w_zero, 2)
            sp.dma_start(m1[0:32, 0:32], a["L2_gnn_W_l1_0"]).then_inc(w_in, 16)
            sp.dma_start(m1[0:32, P:P + 32], a["L2_gnn_W_sc0"]).then_inc(w_in, 16)
            for d in range(3):
                sp.dma_start(m1[32 + d:P:3, 32 + 32 * d:64 + 32 * d], a["L2_gnn_W_l1_1"]).then_inc(w_in, 16)
                sp.dma_start(m1[32 + d:P:3, P + 32 + d:2 * P:3], a["L2_gnn_W_sc1"],
                             allow_slow_non_contiguous=True).then_inc(w_in, 16)
            sp.dma_start(m2[0:32, 0, 0:32], a["L2_gnn_W_l2_A0"]).then_inc(w_in, 16)
            sp.dma_start(m2[0:32, 0, D:D + 1], a["L2_gnn_W_l3_A"]).then_inc(w_in, 16)
            for d in range(3):
                at = 32 + 32 * d
                sp.dma_start(m2[at:at + 32, 0, 0:32], a["L2_gnn_W_l2_B0"]).then_inc(w_in, 16)
                sp.dma_start(m2[at:at + 32, 0, D:D + 1], a["L2_gnn_W_l3_B"]).then_inc(w_in, 16)
                sp.dma_start(m2[at - 32:at, 1, 32 + d:D:3], a["L2_gnn_W_l2_C1"],
                             allow_slow_non_contiguous=True).then_inc(w_in, 16)
                n, at = ((1, 96), (2, 0), (2, 32))[d]
                sp.dma_start(m2[at:at + 32, n, 32 + d:D:3], a["L2_gnn_W_l2_D1"],
                             allow_slow_non_contiguous=True).then_inc(w_in, 16)
            for n in range(TILES):
                sp.wait_ge(f_ready, n + 1)
                sp.dma_start(t["f"][n * P:(n + 1) * P, :], fst[:, n % 4]).then_inc(f_out[n % 4], 16)
            for n in range(4):
                sp.wait_ge(f_out[n], 16 * len(range(n, TILES, 4)))
            sp.sem_inc(f_all, 1)
            wtab = t["w"].rearrange("(e p) f -> e p f", p=P)
            with sp.Fori(0, BODIES) as i:
                for u in range(U):
                    n = U * i + u
                    e = sp.value_load(s["stepE"][0:1, bass.ds(n, 1)], min_val=0, max_val=STEPS - 1)
                    sp.wait_ge(step_done, n + 1)
                    sp.dma_start(wrow[:, u], wtab[bass.ds(e, 1)].rearrange("o p f -> (o p) f")).then_inc(w_row_in[u], 16)
            rows_out = t["x3"].rearrange("(g u p) f -> g p u f", p=P, u=G)
            with sp.Fori(0, GROUPS) as g:
                sp.wait_ge(ln.ready, g + 1)
                sp.dma_start(rows_out[bass.ds(g, 1)].rearrange("o p u f -> (o p) u f"), xout[:]).then_inc(stored, 16)
                sp.wait_ge(stored, 16 * g + 16)
                sp.sem_inc(ln.free, 1)

        @block.gpsimd
        def _(pool):
            pool.wait_ge(f_all, 1)
            with pool.Fori(0, BODIES // 2) as i:
                for h in range(2):
                    pool.wait_ge(idx_ready, 2 * i + h + 1)
                    for u in range(U):
                        pool.wait_ge(step_done, U * (2 * i + h) + u + 1)
                        pool.sem_inc(took, 1)
                        pool.indirect_dma_start(frow[:, u, :], None, t["f"],
                                                bass.IndirectOffsetOnAxis(ap=idx[:, h, u:u + 1], axis=0)).then_inc(gathered[u], 16)

        @block.scalar
        def _(act):
            with act.Fori(0, BODIES // 2) as i:
                for h in range(2):
                    n0 = U * (2 * i + h)
                    act.wait_ge(step_done, n0 + 1)
                    act.copy(idx[:, h], s["srcS"][:, bass.ds(n0, U)]).then_inc(idx_ready, 1)
                    for u in range(U):
                        act.wait_ge(w_row_in[u], 16 * (2 * i + h) + 16)
                        act.wait_ge(msg_ready, n0 + u + 1)
                        for f in range(4):
                            lo = 0 if f == 0 else 64
                            last = act.activation(pb[:, u % 4, f].rearrange("p c w -> p (c w)"), wrow[:, u, lo:lo + 64], ACT.Copy,
                                                  scale=wrow[:, u, D + f:D + f + 1])
                        last.then_inc(pb_ready, 1)
            for n in range(2):
                act.wait_ge(trig, n + 1)
                act.activation(r_[2 + n][:], r_[2 + n][:], ACT.Sin).then_inc(trig_back, 1)
            ln.scalar(act)

        @block.tensor
        def _(pe):
            pe.sem_inc(step_done, U)
            pe.wait_ge(x_in, 32)
            pe.wait_ge(w_in, 16 * 22)

            def features(n):
                pe.wait_ge(xt_ready, n + 1)
                if n >= 2:
                    pe.wait_ge(f_ready, n - 1)
                pe.matmul(ps[:, 2 + n % 2, 0:2 * P], xt[:, n % 2], m1[:], start=True, stop=True).then_inc(f_psum, 1)

            for n in range(TILES):
                if n >= 2:
                    pe.wait_ge(xt_ready, n - 1)
                pe.transpose(ps[:, n % 2, 0:P], x2[:, n], s["ident"][:]).then_inc(xt_psum, 1)
                if n:
                    features(n - 1)
            features(TILES - 1)
            with pe.Fori(0, BODIES) as i:
                for u in range(U):
                    n = U * i + u
                    pe.wait_ge(msg_ready, n + 5)
                    pe.wait_ge(onehot_ready, n + 1)
                    pe.wait_ge(added, n + 1)
                    pe.matmul(ps[:, u % 4, 0:MC], onehot[:, u], msg[:, u % 4], start=True, stop=True).then_inc(step_done, 1)

            def second(n):
                pe.wait_ge(mt_ready, n + 1)
                if n >= 2:
                    pe.wait_ge(c_ready, n - 1)
                for k in range(3):
                    rows = 64 if k == 2 else P
                    last = pe.matmul(ps[:, 6 + n % 2, 0:D + 1], mt[0:rows, n % 2, k], m2[0:rows, k], start=(k == 0), stop=(k == 2))
                last.then_inc(c_psum, 1)

            pe.wait_ge(added, STEPS + 4)
            for n in range(TILES):
                if n >= 2:
                    pe.wait_ge(mt_ready, n - 1)
                for k in range(3):
                    cols = 64 if k == 2 else P
                    last = pe.transpose(ps[0:cols, 4 + n % 2, k * P:(k + 1) * P], acc[:, n, k * P:k * P + cols], s["ident"][:])
                last.then_inc(mt_psum, 1)
                if n:
                    second(n - 1)
            second(TILES - 1)

        @block.vector
        def _(dve):
            do = Chain(dve, own)
            dve.memset(m1[:], 0.0).then_inc(w_zero, 1)
            dve.memset(m2[:], 0.0).then_inc(w_zero, 1)
            dve.sem_inc(added, 4)
            dve.sem_inc(msg_ready, 4)
            do.put(dve.memset(acc[:], 0.0))
            do.put(dve.memset(mt[:], 0.0))
            do(dve.tensor_scalar(rowscale[:], s["part"][:], 32.0, 1.0 / 3.0 ** 0.5 - 1.0, ALU.is_ge, ALU.mult))
            do(dve.tensor_scalar(rowscale[:], rowscale[:], 1.0, None, ALU.add))
            dve.wait_ge(x_in, 32)
            dve.wait_ge(w_in, 16 * 22)
            do(dve.tensor_scalar(fscale[:], attr[:], 1.0 / 32.0 ** 0.5, None, ALU.mult))
            do(dve.tensor_scalar(m2[:, 0], m2[:, 0], rowscale[:], None, ALU.mult))

            def features(n):
                dve.wait_ge(f_psum, n + 1)
                if n >= 4:
                    dve.wait_ge(f_out[n % 4], 16 * (n // 4))
                do.put(dve.tensor_copy(sc[:, n], ps[:, 2 + n % 2, P:2 * P]))
                dve.tensor_scalar(fst[:, n % 4], ps[:, 2 + n % 2, 0:P], fscale[:, n:n + 1], None, ALU.mult).then_inc(f_ready, 1)

            for n in range(TILES):
                dve.wait_ge(xt_psum, n + 1)
                if n >= 2:
                    dve.wait_ge(f_psum, n - 1)
                dve.tensor_copy(xt[:, n % 2], ps[:, n % 2, 0:P]).then_inc(xt_ready, 1)
                if n:
                    features(n - 1)
            features(TILES - 1)

            def add(i, u, tile):
                n = U * i + u
                dve.wait_ge(step_done, n + 1 + U)
                dve.wait_ge(added, n + 4)
                into = acc[:, bass.ds(tile, 1), :].rearrange("p o c -> p (o c)")
                dve.tensor_tensor(into, into, ps[:, u % 4, 0:MC], ALU.add).then_inc(added, 1)

            with dve.Fori(0, BODIES) as i:
                tiles = []
                for u in range(U):
                    n = U * i + u
                    if u % 4 == 0:
                        tiles += node_tiles(dve, s, 2 * i + u // 4)
                    dve.wait_ge(step_done, n + 1)
                    dve.tensor_scalar(onehot[:, u], s["iota"][:], s["dstS"][:, bass.ds(n, 1)], None,
                                      ALU.is_equal).then_inc(onehot_ready, 1)
                    dve.wait_ge(step_done, n + 5)
                    dve.wait_ge(gathered[u], 16 * i + 16)
                    dve.wait_ge(pb_ready, n + 1)
                    p4, m = pb[:, u % 4], msg[:, u % 4]
                    f4 = frow[:, u].rearrange("p (k w) -> p k w", k=4)
                    dve.tensor_tensor(m[:, 0:P].rearrange("p (k w) -> p k w", k=4), p4[:, :, 1], f4, ALU.mult)
                    dve.tensor_tensor(m[:, P:P + 96].rearrange("p (k w) -> p k w", k=3), p4[:, 1:4, 0],
                                      f4[:, 0].unsqueeze(1).broadcast_to([P, 3, 32]), ALU.mult)
                    dve.tensor_tensor(m[:, P + 96:MC].rearrange("p (k w) -> p k w", k=3),
                                      p4[:, 0, 0].unsqueeze(1).broadcast_to([P, 3, 32]), f4[:, 1:4], ALU.mult).then_inc(msg_ready, 1)
                    if u >= 2:
                        add(i, u - 2, tiles[u - 2])
                for u in (U - 2, U - 1):
                    add(i, u, tiles[u])

            def products(n):
                dve.wait_ge(c_psum, n + 1)
                do.put(dve.tensor_copy(ang[:, n:n + 1], ps[:, 6 + n % 2, D:D + 1]))
                dve.tensor_copy(cc[:, n, 0:D], ps[:, 6 + n % 2, 0:D]).then_inc(c_ready, 1)

            for n in range(TILES):
                dve.wait_ge(mt_psum, n + 1)
                if n >= 2:
                    dve.wait_ge(c_psum, n - 1)
                dve.tensor_copy(mt[:, n % 2, 0:2].rearrange("p k c -> p (k c)"), ps[:, 4 + n % 2, 0:2 * P])
                dve.tensor_copy(mt[0:64, n % 2, 2], ps[0:64, 4 + n % 2, 2 * P:3 * P]).then_inc(mt_ready, 1)
                if n:
                    products(n - 1)
            products(TILES - 1)
            dve.wait_ge(c_ready, TILES)
            do.sync()
            k_, rem, sn, cs = r_
            do(dve.tensor_scalar(attr[:], attr[:], 1.0 / 32, None, ALU.mult))
            do(dve.tensor_tensor(ang[:], ang[:], attr[:], ALU.mult))
            do(dve.tensor_scalar(ang[:], ang[:], 0.1, None, ALU.mult))
            magic = 1.5 * 2.0 ** 23
            do(dve.tensor_scalar(k_[:], ang[:], float(1 / (2 * np.pi)), magic, ALU.mult, ALU.add))
            do(dve.tensor_scalar(k_[:], k_[:], -magic, None, ALU.add))
            turn = 2 * np.pi
            hi = 6.28125
            mid = float(np.round((turn - hi) * 2 ** 20) / 2 ** 20)
            lo = turn - hi - mid
            do(dve.scalar_tensor_tensor(rem[:], k_[:], -hi, ang[:], ALU.mult, ALU.add))
            do(dve.scalar_tensor_tensor(rem[:], k_[:], -mid, rem[:], ALU.mult, ALU.add))
            do(dve.scalar_tensor_tensor(rem[:], k_[:], -lo, rem[:], ALU.mult, ALU.add))
            pi = float(np.nextafter(np.float32(np.pi), np.float32(0)))
            do(dve.tensor_scalar(sn[:], rem[:], -pi, pi, ALU.max, ALU.min))
            dve.sem_inc(trig, 1)
            do(dve.tensor_scalar(rem[:], rem[:], float(np.pi / 2), None, ALU.add))
            do(dve.tensor_scalar(k_[:], rem[:], float(np.pi), -float(turn), ALU.is_gt, ALU.mult))
            do(dve.tensor_tensor(rem[:], rem[:], k_[:], ALU.add))
            do(dve.tensor_scalar(cs[:], rem[:], -pi, pi, ALU.max, ALU.min))
            dve.sem_inc(trig, 1)
            dve.wait_ge(trig_back, 2)
            do.put(dve.tensor_tensor(cs[:], cs[:], fscale[:], ALU.mult))
            do(dve.tensor_tensor(sn[:], sn[:], attr[:], ALU.mult))
            for n in range(TILES):
                do.put(dve.scalar_tensor_tensor(x2[:, n], sc[:, n], cs[:, n:n + 1], x2[:, n], ALU.mult, ALU.add))
            do.sync()
            for n in range(TILES):
                do.put(dve.scalar_tensor_tensor(x2[:, n], cc[:, n, 0:D], sn[:, n:n + 1], x2[:, n], ALU.mult, ALU.add))
            do.sync()
            ln.vector(dve, x2, lambda g, u: xout[:, u])


def gat(nc, a, t, s, out):
    NEG = 0.2
    heads, cols = 4, D // 4
    with ExitStack() as ctx:
        def sb(name, shape, dt=F32):
            return ctx.enter_context(nc.sbuf_tensor(f"gt_{name}", shape, dt))

        sem = Semaphores(nc, ctx, "gt_")
        ps = ctx.enter_context(nc.psum_tensor("gt_ps", [P, 8, 512], F32))
        x3 = sb("x3", [P, TILES, D])
        xt = sb("xt", [P, 2, P])
        wc = sb("wc", [P, HW])
        att = sb("att", [P, 2, D])
        bias, gain, shift = (sb(n, [P, D]) for n in ("bias", "gain", "shift"))
        hrow = sb("hrow", [P, TILES, HW])
        own_row = sb("own_row", [P, TILES, HW + D])
        res = sb("res", [P, TILES, D])
        rd = Rounds(ctx, nc, sem, s, "gt", t["edge"], t["h"], HW, EF)
        ln = [LayerNorm(ctx, nc, lambda n, k=k: sem(f"{k}_{n}"), f"gt_{k}") for k in ("inner", "outer")]
        adst, loop, ae_sum = (sb(n, [P, G, heads]) for n in ("adst", "loop", "ae_sum"))
        alpha = sb("alpha", [P, 2, G, heads])
        scores = sb("scores", [P, 3, G, heads])
        top = sb("top", [P, G, heads])
        below = sb("below", [P, 3, G, heads])
        ex = sb("ex", [P, 3, G, heads])
        ae = sb("ae", [P, 2, G, heads])
        den = sb("den", [P, G, heads])
        acc = sb("acc", [P, G, D])
        prod = sb("prod", [P, 2, G, D])
        valid = sb("valid", [P, 2, G])
        limit_ = sb("limit", [P, 2, G])
        dg = sb("dg", [P, G])
        rdeg = sb("rdeg", [P, G])
        kk = sb("kk", [P, 2])

        x_in, w_in, own = sem("x_in"), sem("w_in"), sem("own")
        xt_psum, xt_ready, h_psum, h_ready = sem("xt_psum"), sem("xt_ready"), sem("h_psum"), sem("h_ready")
        w_ready, h_out, nodes_in = sem("w_ready"), sem("h_out"), sem("nodes_in")
        grp, bod = sem("group_own"), sem("body_own")
        below_ready, ex_ready = sem("below_ready"), sem("ex_ready")
        scattered = sem("scattered")
        block = ctx.enter_context(nc.Block())
        H_OUT = 16 * (2 * GROUPS + 1)

        @block.sync
        def _(sp):
            sp.dma_start(x3[:], t["x3"].rearrange("(t p) d -> p t d", p=P)).then_inc(x_in, 16)
            sp.dma_start(wc[:, 0:D], a["L3_gnn_W_lin"]).then_inc(w_in, 16)
            for n, name in enumerate(("att_src", "att_dst")):
                sp.dma_start(att[:, n], a["L3_gnn_" + name].rearrange("h c -> (h c)").partition_broadcast(P)).then_inc(w_in, 16)
            for tile, name in ((bias, "bias"), (gain, "ln_g"), (shift, "ln_b")):
                sp.dma_start(tile[:], a["L3_gnn_" + name].partition_broadcast(P)).then_inc(w_in, 16)
            by_group = t["h"].rearrange("(g u p) f -> g p u f", p=P, u=G)
            own_by_group = t["hx"].rearrange("(g u p) f -> g p u f", p=P, u=G)
            sp.wait_ge(x_in, 16)
            sp.dma_start(t["hx"].rearrange("(t p) f -> p t f", p=P)[:, :, HW:HW + D], x3[:]).then_inc(h_out, 16)
            for g in range(GROUPS):
                sp.wait_ge(h_ready, G * (g + 1))
                rows = hrow[:, g * G:(g + 1) * G]
                sp.dma_start(by_group[g], rows).then_inc(h_out, 16)
                sp.dma_start(own_by_group[g][:, :, 0:HW], rows).then_inc(h_out, 16)

        @block.gpsimd
        def _(pool):
            pool.wait_ge(h_out, H_OUT)
            for n in range(TILES):
                pool.indirect_dma_start(own_row[:, n, :], None, t["hx"],
                                        bass.IndirectOffsetOnAxis(ap=s["perm"][:, n:n + 1], axis=0)).then_inc(nodes_in, 16)
            rd.gather(pool)
            for n in range(TILES):
                real = min(P, N - n * P)
                if n % G == 0:
                    pool.wait_ge(ln[1].ready, n // G + 1)
                pool.indirect_dma_start(out[:, :], bass.IndirectOffsetOnAxis(ap=s["perm"][0:real, n:n + 1], axis=0),
                                        res[0:real, n, :], None).then_inc(scattered, 16)
            pool.wait_ge(scattered, 16 * TILES)

        @block.scalar
        def _(act):
            with act.Fori(0, GROUPS) as g:
                q, q_before, chunks, c_before = rd.group(act, g)
                with act.Fori(0, q) as j:
                    for half in range(2):
                        act.wait_ge(below_ready, (q_before + j) * 2 + g + half + 1)
                        act.activation(ex[:], below[:], ACT.Exp).then_inc(ex_ready, 1)
                act.wait_ge(below_ready, (q_before + q) * 2 + g + 1)
                act.activation(ex[:], below[:], ACT.Exp).then_inc(ex_ready, 1)
            ln[0].scalar(act)
            ln[1].scalar(act)

        @block.tensor
        def _(pe):
            pe.wait_ge(x_in, 16)

            def project(n):
                pe.wait_ge(xt_ready, n + 1)
                if n >= 2:
                    pe.wait_ge(h_ready, n - 1)
                pe.matmul(ps[:, 2 + n % 2, 0:HW], xt[:, n % 2], wc[:], start=True, stop=True).then_inc(h_psum, 1)

            for n in range(TILES):
                if n >= 2:
                    pe.wait_ge(xt_ready, n - 1)
                pe.transpose(ps[:, n % 2, 0:P], x3[:, n], s["ident"][:]).then_inc(xt_psum, 1)
                if n == 1:
                    pe.wait_ge(w_ready, 1)
                if n:
                    project(n - 1)
            project(TILES - 1)

        @block.vector
        def _(dve):
            do = Chain(dve, own)
            dve.wait_ge(w_in, 16 * 6)
            do.put(dve.tensor_tensor(prod[:, 0, 0], wc[:, 0:D], att[:, 0], ALU.mult))
            do(dve.tensor_tensor(prod[:, 0, 1], wc[:, 0:D], att[:, 1], ALU.mult))
            do(dve.tensor_reduce(wc[:, D:HW], prod[:, 0, 0:2].rearrange("p n (h c) -> p (n h) c", c=cols), AX_X, ALU.add))
            dve.sem_inc(w_ready, 1)

            def project(n):
                dve.wait_ge(h_psum, n + 1)
                dve.tensor_copy(hrow[:, n], ps[:, 2 + n % 2, 0:HW]).then_inc(h_ready, 1)

            for n in range(TILES):
                dve.wait_ge(xt_psum, n + 1)
                if n >= 2:
                    dve.wait_ge(h_psum, n - 1)
                dve.tensor_copy(xt[:, n % 2], ps[:, n % 2, 0:P]).then_inc(xt_ready, 1)
                if n:
                    project(n - 1)
            project(TILES - 1)

            dve.wait_ge(nodes_in, 16 * TILES)
            dve.sem_inc(rd.raw_free, 1)
            dve.sem_inc(rd.round_done, R)
            GROUP_OPS, HALF_OPS = 27, 23
            pair = [P, 2, G]
            four = [P, 2, G, heads]

            def wide(x):
                return x.rearrange("p u h -> p (u h)").unsqueeze(2).broadcast_to([P, G * heads, cols])

            limit = dve.alloc_register("gt_chunk_end")
            by_head = "p u (h c) -> p (u h) c"
            with dve.Fori(0, GROUPS) as g:
                q, q_before, chunks, c_before = rd.group(dve, g)
                do = Chain(dve, grp, g * GROUP_OPS, rd.took)
                mine = bass.ds(g * G, G)
                do.put(dve.tensor_copy(adst[:], own_row[:, mine, D + heads:HW]))
                do.put(dve.tensor_tensor(loop[:], own_row[:, mine, D:D + heads], own_row[:, mine, D + heads:HW], ALU.add))
                do.put(dve.tensor_copy(dg[:], s["sdeg"][:, mine]))
                do.put(dve.tensor_copy(rd.bits[:], s["sbit"][:, :, mine]))
                do.put(dve.memset(acc[:], 0.0))
                do.put(dve.memset(den[:], 0.0))
                do.put(dve.memset(ae_sum[:], 0.0))
                do.put(dve.memset(scores[:, 2], -BIG))
                do.put(dve.memset(kk[:, 0:1], 0.0))
                do(dve.memset(kk[:, 1:2], 1.0))
                do(dve.tensor_scalar(rdeg[:], dg[:], 1.0, None, ALU.max))
                do(dve.reciprocal(rdeg[:], rdeg[:]))
                with dve.Fori(0, chunks) as c:
                    rd.shift(dve, c_before + c)
                    lo, hi = rd.bodies(dve, limit, c, q)
                    with dve.Fori(lo, hi) as j:
                        place = dve.snap((j - lo) * R).with_bounds(min_val=0, max_val=RUN - R)
                        do_b = Chain(dve, bod, (q_before + j) * (2 * HALF_OPS))
                        for half in range(2):
                            start = do_b.n
                            rows = rd.rows[:, 2 * half:2 * half + 2]
                            for r in range(2):
                                dve.wait_ge(rd.gathered[2 * half + r], (q_before + j + 1) * (16 * G))
                            do_b(dve.tensor_copy(ae[:], rd.edges[:, :, bass.ds(place + 2 * half, 2), 1:EF]
                                                 .rearrange("p u r f -> p r u f")))
                            do_b.put(dve.tensor_tensor(valid[:], dg[:].unsqueeze(1).broadcast_to(pair),
                                                       kk[:].unsqueeze(2).broadcast_to(pair), ALU.is_gt))
                            do_b(dve.tensor_tensor(alpha[:], rows[:, :, :, D:D + heads], ae[:], ALU.add))
                            valid4 = valid[:].unsqueeze(3).broadcast_to(four)
                            do_b.put(dve.tensor_scalar(kk[:], kk[:], 2.0, None, ALU.add))
                            do_b.put(dve.tensor_tensor(ae[:], ae[:], valid4, ALU.mult))
                            do_b.put(dve.tensor_scalar(limit_[:], valid[:], 2.0 * BIG, -BIG, ALU.mult, ALU.add))
                            do_b(dve.tensor_tensor(alpha[:], alpha[:], adst[:].unsqueeze(1).broadcast_to(four), ALU.add))
                            do_b.put(dve.tensor_tensor(ae_sum[:], ae_sum[:], ae[:, 0], ALU.add))
                            do_b(dve.scalar_tensor_tensor(alpha[:], alpha[:], NEG, alpha[:], ALU.mult, ALU.max))
                            do_b.put(dve.tensor_tensor(ae_sum[:], ae_sum[:], ae[:, 1], ALU.add))
                            do_b(dve.tensor_tensor(scores[:, 0:2], alpha[:], limit_[:].unsqueeze(3).broadcast_to(four), ALU.min))
                            do_b(dve.tensor_reduce(top[:].rearrange("p u h -> p (u h)"),
                                                   scores[:].rearrange("p r u h -> p (u h) r"), AX_X, ALU.max))
                            do_b(dve.tensor_tensor(below[:], scores[:], top[:].unsqueeze(1).broadcast_to([P, 3, G, heads]),
                                                   ALU.subtract))
                            dve.sem_inc(below_ready, 1)
                            do_b.put(dve.tensor_copy(scores[:, 2], top[:]))
                            dve.wait_ge(ex_ready, (q_before + j) * 2 + g + half + 1)
                            do_b.put(dve.tensor_tensor(acc[:].rearrange(by_head, c=cols), acc[:].rearrange(by_head, c=cols),
                                                       wide(ex[:, 2]), ALU.mult))
                            do_b.put(dve.tensor_tensor(den[:], den[:], ex[:, 2], ALU.mult))
                            do_b(dve.tensor_tensor(ex[:, 0:2], ex[:, 0:2], valid4, ALU.mult))
                            for r in range(2):
                                do_b.put(dve.tensor_tensor(prod[:, r].rearrange(by_head, c=cols).rearrange("p (u h) c -> p u h c", h=heads),
                                                           rows[:, r, :, 0:D].rearrange("p u (h c) -> p u h c", c=cols),
                                                           ex[:, r].unsqueeze(3).broadcast_to([P, G, heads, cols]), ALU.mult))
                                do_b(dve.tensor_tensor(den[:], den[:], ex[:, r], ALU.add))
                                dve.sem_inc(rd.round_done, 1)
                            for r in range(2):
                                do_b(dve.tensor_tensor(acc[:], acc[:], prod[:, r], ALU.add))
                            assert do_b.n - start == HALF_OPS, do_b.n - start
                do(dve.tensor_tensor(ae_sum[:], ae_sum[:], rdeg[:].unsqueeze(2).broadcast_to([P, G, heads]), ALU.mult))
                do(dve.tensor_tensor(loop[:], loop[:], ae_sum[:], ALU.add))
                do(dve.scalar_tensor_tensor(loop[:], loop[:], NEG, loop[:], ALU.mult, ALU.max))
                do(dve.tensor_tensor(top[:], loop[:], scores[:, 2], ALU.max))
                do.put(dve.tensor_tensor(below[:, 0:2], loop[:].unsqueeze(1).broadcast_to(four),
                                         top[:].unsqueeze(1).broadcast_to(four), ALU.subtract))
                do(dve.tensor_tensor(below[:, 2], scores[:, 2], top[:], ALU.subtract))
                dve.sem_inc(below_ready, 1)
                dve.wait_ge(ex_ready, (q_before + q) * 2 + g + 1)
                dve.sem_inc(rd.took, 1)
                do.put(dve.tensor_tensor(acc[:].rearrange(by_head, c=cols), acc[:].rearrange(by_head, c=cols),
                                         wide(ex[:, 2]), ALU.mult))
                do.put(dve.tensor_tensor(prod[:, 0].rearrange("p u (h c) -> p u h c", c=cols),
                                         own_row[:, mine, 0:D].rearrange("p u (h c) -> p u h c", c=cols),
                                         ex[:, 0].unsqueeze(3).broadcast_to([P, G, heads, cols]), ALU.mult))
                do(dve.tensor_tensor(den[:], den[:], ex[:, 2], ALU.mult))
                do(dve.tensor_tensor(den[:], den[:], ex[:, 0], ALU.add))
                do.put(dve.tensor_tensor(acc[:], acc[:], prod[:, 0], ALU.add))
                do(dve.reciprocal(den[:], den[:]))
                do(dve.tensor_tensor(acc[:].rearrange(by_head, c=cols), acc[:].rearrange(by_head, c=cols), wide(den[:]), ALU.mult))
                do.put(dve.tensor_tensor(prod[:, 1], own_row[:, mine, HW:HW + D], bias[:].unsqueeze(1).broadcast_to([P, G, D]), ALU.add))
                do.sync()
                do.put(dve.tensor_tensor(res[:, mine], acc[:], prod[:, 1], ALU.add))
                do.sync()
                assert do.n == GROUP_OPS, do.n
            for k in range(2):
                dve.sem_inc(ln[k].free, GROUPS)
            into = lambda g, u: res[:, bass.ds(g * G + u, 1)].rearrange("p o d -> p (o d)")
            ln[0].vector(dve, res, into)
            do = Chain(dve, own, 3)
            every = [P, TILES, D]
            do(dve.tensor_tensor(res[:], res[:], gain[:].unsqueeze(1).broadcast_to(every), ALU.mult))
            do.put(dve.tensor_tensor(own_row[:, :, HW:HW + D], own_row[:, :, HW:HW + D], shift[:].unsqueeze(1).broadcast_to(every), ALU.add))
            do.sync()
            do(dve.tensor_tensor(res[:], res[:], own_row[:, :, HW:HW + D], ALU.add))
            ln[1].vector(dve, res, into)


def lay_out(inputs):
    def pad(x, shape, value=0):
        out = np.full(shape, value, x.dtype)
        out[tuple(slice(0, n) for n in x.shape)] = x
        return out

    v = {k: np.asarray(x) for k, x in inputs.items()}
    x = pad(v["x"], (NP, D))
    arrays = {
        "x": x,
        "xT": np.ascontiguousarray(x.T),
        "src": pad(v["src"], (EP,)),
        "dst": pad(v["dst"], (EP,), DST_PAD),
        "ea16T": np.ascontiguousarray(pad(v["edge_attr_16"], (EBP + 2 * EB, 16)).reshape(-1, P, 8, 16)
                                      .transpose(2, 3, 0, 1).reshape(P, -1)),
        "ea64T": np.ascontiguousarray(pad(v["edge_attr_64"], ((WTILES + 2 * WB) * P, 64)).reshape(-1, 2, P, 64)
                                      .transpose(1, 3, 0, 2).reshape(P, -1)),
        "ea4": pad(v["edge_attr_4"], ((WTILES + 2 * WB) * P, 4)),
        "attr": pad(v["node_vec1"], (NP, 1)),
    }
    for name, x in v.items():
        if name[:2] in ("L0", "L2", "L3"):
            arrays[name] = x
    return arrays


def kernel(**inputs):
    import concourse.bacc as bacc
    from concourse.bass_utils import run_bass_kernel_spmd

    nc = bacc.Bacc("TRN2", target_bir_lowering=False, num_devices=1)
    arrays = lay_out(inputs)
    args = {name: nc.dram_tensor(f"in_{name}", x.shape, mybir.dt.from_np(x.dtype), kind="ExternalInput").ap()
            for name, x in arrays.items()}
    out = nc.dram_tensor("out", (N, D), F32, kind="ExternalOutput").ap()
    build(nc, args, out)
    r = run_bass_kernel_spmd(nc, [{f"in_{name}": x for name, x in arrays.items()}], core_ids=[0])
    return r.results[0]["out"]
```
